# Optimizing a Trainium2 kernel written in Bass

```python
import numpy as np
import jax
import jax.numpy as jnp

def _softmax(x, axis=-1):
    return jax.nn.softmax(x, axis=axis)

def _gelu(x):
    return jax.nn.gelu(x, approximate=True)

def _silu(x):
    return jax.nn.silu(x)

def _sigmoid(x):
    return jax.nn.sigmoid(x)

def _layernorm(x, axis=-1, eps=1e-05):
    m = jnp.mean(x, axis=axis, keepdims=True)
    v = jnp.var(x, axis=axis, keepdims=True)
    return (x - m) / jnp.sqrt(v + eps)

def _scatter_add(tgt, idx, src, axis=0):
    return tgt.at[idx].add(src)

def _segment_sum(src, seg, n):
    return jax.ops.segment_sum(src, seg, n)
kernel_name = 'mk_conv_preact_d2_conv_nhwc384_r4_81de7d'

def setup_inputs(seed: int=0):
    np.random.seed(seed)
    _w = jnp.asarray

    def _rec_inputs():
        import jax
        import jax.numpy as jnp
        _gk = jax.random.key(seed)
        x = -0.0001476 + 0.9999 * jax.random.normal(jax.random.fold_in(_gk, 1), (32, 56, 56, 96), jnp.float32)
        return x
    x = _rec_inputs()

    def _L0_conv_setup():
        import jax, jax.numpy as jnp
        import numpy as np
        B, H, W, C = (32, 56, 56, 96)
        HEADS, K, PAD, STRIDE = (12, 3, 1, 2)
        KK = K * K
        key = jax.random.key(seed)
        ks = jax.random.split(key, 5)
        x = jax.random.normal(ks[0], (B, H, W, C), jnp.float32)
        W_v = jax.random.normal(ks[1], (C, C), jnp.float32) / np.float32(np.sqrt(C))
        W_a = jax.random.normal(ks[2], (C, KK * KK * HEADS), jnp.float32) / np.float32(np.sqrt(C))
        b_a = jnp.zeros((KK * KK * HEADS,), jnp.float32)
        W_o = jax.random.normal(ks[3], (C, C), jnp.float32) / np.float32(np.sqrt(C))
        b_o = jnp.zeros((C,), jnp.float32)
        return {'x': x, 'W_v': W_v, 'W_a': W_a, 'b_a': b_a, 'W_o': W_o, 'b_o': b_o}
    _L0_conv_all = _L0_conv_setup()
    _L0_conv_in = {k: v for k, v in _L0_conv_all.items() if k in ('W_v', 'W_a', 'b_a', 'W_o', 'b_o')}
    del _L0_conv_all

    def _L1_conv_setup():
        import jax, jax.numpy as jnp
        import numpy as np
        from jax import lax
        key = jax.random.key(seed)
        k1, k2 = jax.random.split(key)
        x = jax.random.normal(k1, (16, 28, 28, 96), dtype=jnp.float32)
        w = jax.random.normal(k2, (3, 3, 96, 1), dtype=jnp.float32)
        return {'x': x, 'w': w}
    _L1_conv_all = _L1_conv_setup()
    _L1_conv_in = {k: v for k, v in _L1_conv_all.items() if k in ('w',)}
    del _L1_conv_all
    return {'x': x, 'L0_conv_W_v': _L0_conv_in['W_v'], 'L0_conv_W_a': _L0_conv_in['W_a'], 'L0_conv_b_a': _L0_conv_in['b_a'], 'L0_conv_W_o': _L0_conv_in['W_o'], 'L0_conv_b_o': _L0_conv_in['b_o'], 'L1_conv_w': _L1_conv_in['w']}

def reference(x, L0_conv_W_v, L0_conv_W_a, L0_conv_b_a, L0_conv_W_o, L0_conv_b_o, L1_conv_w):
    import jax
    import jax.numpy as jnp

    def _L0_conv_ref(x, W_v, W_a, b_a, W_o, b_o):
        import jax, jax.numpy as jnp
        import numpy as np
        B, H, W, C = (32, 56, 56, 96)
        HEADS, K, PAD, STRIDE = (12, 3, 1, 2)
        KK = K * K
        b, hh, ww, c = x.shape
        hd = c // HEADS
        h, w = (-(-hh // STRIDE), -(-ww // STRIDE))
        scale = hd ** (-0.5)
        ii = (jnp.arange(h) * STRIDE)[:, None] + jnp.arange(K)
        jj = (jnp.arange(w) * STRIDE)[:, None] + jnp.arange(K)
        v = x @ W_v
        v_pad = jnp.pad(v, ((0, 0), (PAD, PAD), (PAD, PAD), (0, 0)))
        v_patch = v_pad[:, ii[:, :, None, None], jj[None, None, :, :], :]
        v_un = v_patch.transpose(0, 1, 3, 2, 4, 5).reshape(b, h * w, KK, HEADS, hd).transpose(0, 3, 1, 2, 4)
        x_pool = x.reshape(b, h, STRIDE, w, STRIDE, c).mean(axis=(2, 4))
        a = x_pool @ W_a + b_a
        a = a.reshape(b, h * w, HEADS, KK, KK).transpose(0, 2, 1, 3, 4)
        a = jax.nn.softmax(a * scale, axis=-1)
        out = jnp.einsum('bnpqk,bnpkd->bnpqd', a, v_un)
        out = out.transpose(0, 2, 3, 1, 4).reshape(b, h, w, K, K, c).transpose(0, 1, 3, 2, 4, 5)
        folded = jnp.zeros((b, hh + 2 * PAD, ww + 2 * PAD, c), x.dtype)
        folded = folded.at[:, ii[:, :, None, None], jj[None, None, :, :], :].add(out)
        y = folded[:, PAD:PAD + hh, PAD:PAD + ww, :]
        return y @ W_o + b_o

    def _L1_conv_ref(x, w):
        import jax, jax.numpy as jnp
        import numpy as np
        from jax import lax
        kh, kw, C, mult = w.shape
        w_clip = jnp.clip(w, -1.0, 1.0)
        binary_kernel = w_clip + lax.stop_gradient(jnp.sign(w_clip) - w_clip)
        k = binary_kernel.reshape(kh, kw, 1, C * mult)
        out = lax.conv_general_dilated(x, k, window_strides=(1, 1), padding='SAME', rhs_dilation=(1, 1), dimension_numbers=('NHWC', 'HWIO', 'NHWC'), feature_group_count=C)
        return out

    def _gn(v, G=32, eps=1e-05):
        B_, H_, W_, C_ = v.shape
        g = v.reshape(B_, H_, W_, G, C_ // G)
        m = jnp.mean(g, axis=(1, 2, 4), keepdims=True)
        s = jnp.var(g, axis=(1, 2, 4), keepdims=True)
        return ((g - m) / jnp.sqrt(s + eps)).reshape(v.shape)

    def _ln_c(v, eps=1e-06):
        m = jnp.mean(v, axis=-1, keepdims=True)
        s = jnp.var(v, axis=-1, keepdims=True)
        return (v - m) / jnp.sqrt(s + eps)

    def _ln_t(v, eps=1e-05):
        m = jnp.mean(v, axis=-1, keepdims=True)
        s = jnp.var(v, axis=-1, keepdims=True)
        return (v - m) / jnp.sqrt(s + eps)

    def _to_tokens(v):
        B_, H_, W_, C_ = v.shape
        return v.reshape(B_, H_ * W_, C_)

    def _from_tokens(t, like):
        return t.reshape(like.shape)
    x = x + _L0_conv_ref(_gn(x), L0_conv_W_v, L0_conv_W_a, L0_conv_b_a, L0_conv_W_o, L0_conv_b_o)
    x = x + _L1_conv_ref(_gn(x), L1_conv_w)
    return x

_drawn_inputs = setup_inputs


def setup_inputs(seed=0):
    import zlib

    import numpy as np

    out = dict(_drawn_inputs(seed))
    spreads = {'L0_conv_b_a': (0.0, 0.58), 'L0_conv_b_o': (0.0, 0.1)}
    factors = {}
    for name, (base, spread) in spreads.items():
        noise = np.random.default_rng([zlib.crc32(name.encode()), seed]).standard_normal(out[name].shape)
        drawn = base * np.exp(spread * noise) if base else spread * noise
        out[name] = jnp.asarray(drawn.astype(out[name].dtype))
    for name, factor in factors.items():
        out[name] = (out[name] * factor).astype(out[name].dtype)
    return out
```

```python
import concourse.bass as bass
from concourse import mybir
from contextlib import ExitStack

BATCH, SIDE, CH = 32, 56, 96
HEADS, DIM, TAPS = 12, 8, 3
GROUP = 3
WIN = SIDE // 2
GRID = WIN + 1
PIX = SIDE * SIDE
PAD_P = SIDE + 2
PAD_V = SIDE + 3
TP, TT = 112, PIX // 112
HALF = WIN // 2
UNIT = HALF * WIN
ROWS = (HALF + 1, HALF)
PIX0 = (0, SIDE // 2 - 1)
PIXN = (SIDE // 2 + 2, SIDE // 2 + 1)
V_ROWS = 2 * (HALF - 1) + 5
KK = TAPS * TAPS
QN = KK * HEADS
PN = TAPS * HEADS
CHUNK = 448
SCALE = float(DIM) ** -0.5

AXIS = {
    0: [(0, [(0, 1, 0)]), (1, [(0, 1, 1)]), (2, [(0, 1, 2)])],
    1: [(0, [(0, 2, 0)]), (1, [(0, 2, 1)]), (2, [(0, 2, 2), (1, 0, 0)]), (3, [(1, 0, 1)]), (4, [(1, 0, 2)])],
}
CLASSES = [(1, 1), (1, 0), (0, 1), (0, 0)]
TERMS = [(c, rv, cv, [(r, q) for r in rows for q in cols])
         for c, (pr, pc) in enumerate(CLASSES) for rv, rows in AXIS[pr] for cv, cols in AXIS[pc]]
SLOTS = len(TERMS) // 2
LAST = [max(n for n, t in enumerate(TERMS) if t[0] == c) // 2 for c in range(4)]
BODY = 2 * SLOTS
LAG = 2
PRODUCTS = 4
V_CUTS = ((0, 8, 16, 23, 30), (0, 8, 15, 22, 29))

V, LOG, IN, OUT, GA, GB = "values", "logits", "in", "out", "mean", "var"
USES = sorted(
    [(0 + k, V, 1, k) for k in range(4)] + [(8, GA, 2, 0), (10, GB, 2, 0)]
    + [(7 + k, IN, 0, k) for k in range(7)] + [(16, GA, 1, 0), (17, GB, 1, 0)]
    + [(22 + k, LOG, 0, k) for k in range(KK)]
    + [(SLOTS + k, V, 0, k) for k in range(4)]
    + [(52 + k // 2, OUT, 0, k) for k in range(7)]
    + [(SLOTS + 22 + k, LOG, 1, k) for k in range(KK)], key=lambda u: u[0])
N_USES = len(USES)
assert N_USES % 2 == 0


def use_no(kind, which, k):
    return next(n for n, u in enumerate(USES) if u[1:] == (kind, which, k))


TAP_SLOTS = [11, 12, 18, 19, 24, 25, 27, 28, 35, 36, 40, 41, 43, 44, 46, 47, 49, 50]


def upto(per_body, i, n):
    return (i + 1) * per_body + n


def build_program(nc, x, W_v, W_a, b_a, W_o, b_o, w_conv, ident, group, select, out):
    F32, BF16 = mybir.dt.float32, mybir.dt.bfloat16
    ALU, ACT, AX = mybir.AluOpType, mybir.ActivationFunctionType, mybir.AxisListType
    ctx = ExitStack()
    with ctx:
        def sb(name, shape, dt=F32):
            return ctx.enter_context(nc.sbuf_tensor(name, shape, dt))

        def sem(name):
            return ctx.enter_context(nc.semaphore(name))

        idn = sb("idn", [TP, TP])
        grp = sb("grp", [CH, CH])
        sel = sb("sel", [3 * PN, TAPS, CH], BF16)
        wv = sb("wv", [CH, CH])
        wo = sb("wo", [CH, CH])
        wa = sb("wa", [CH, KK, KK, HEADS])
        ba = sb("ba", [QN, KK])
        bo = sb("bo", [CH, 1])
        wc = sb("wc", [CH, KK])
        sg = sb("sg", [CH, KK])
        sg2 = sb("sg2", [CH, KK])
        half_neg = sb("half_neg", [CH, 1])
        eps = sb("eps", [CH, 1])
        tok_in = sb("tok_in", [TP, TT, CH])
        tok_out = sb("tok_out", [TP, TT, CH])
        X0 = sb("X0", [CH, PIX])
        XN = sb("XN", [CH, PIXN[0], SIDE])
        X1 = sb("X1", [CH, SIDE, SIDE])
        ACC = sb("ACC", [CH, SIDE, SIDE])
        XP = sb("XP", [CH, PAD_P, PAD_P])
        VAL = [sb(f"VAL{h}", [CH, V_ROWS, PAD_V]) for h in range(2)]
        pc = sb("pc", [CH, PIXN[0], WIN])
        pooled = sb("pooled", [CH, ROWS[0], WIN])
        att = sb("att", [QN, KK * ROWS[0] * WIN])
        top = sb("top", [QN, ROWS[0] * WIN])
        parts = [sb(f"part{p}", [QN, KK, ROWS[0], GRID], BF16) for p in range(3)]
        stack = [sb(f"stack{h}", [3 * PN, TAPS, KK, HALF + 1, GRID], BF16) for h in range(2)]
        prod = sb("prod", [CH, PRODUCTS, 2, UNIT])
        stats = sb("stats", [CH, 2, 7, 6])
        mv = sb("mv", [CH, 2, 2])
        nmean = sb("nmean", [CH, 2])
        dev = sb("dev", [CH, 2])
        dev2 = sb("dev2", [CH, 2])
        gvar = sb("gvar", [CH, 2])
        gve = sb("gve", [CH, 2])
        rstd = sb("rstd", [CH, 2])
        shift = sb("shift", [CH, 2])

        bc = [ctx.enter_context(nc.psum_tensor(f"bc{b}", [128, 2, 512], F32)) for b in range(2)]
        acc = [ctx.enter_context(nc.psum_tensor(f"acc{b}", [128, 512], F32)) for b in range(2)]
        side = [ctx.enter_context(nc.psum_tensor(f"side{b}", [128, 512], F32)) for b in range(2)]

        weights_in = sem("weights_in")
        weights_up = sem("weights_up")
        pads_zero = sem("pads_zero")
        bcast_full = sem("bcast_full")
        prod_ready = sem("prod_ready")
        summed = sem("summed")
        y_added = sem("y_added")
        side_full = sem("side_full")
        side_read = sem("side_read")
        xn_ready = sem("xn_ready")
        pool_step = sem("pool_step")
        soft_step = sem("soft_step")
        exp_done = sem("exp_done")
        hi_done = sem("hi_done")
        rest_done = sem("rest_done")
        mid_done = sem("mid_done")
        lo_done = sem("lo_done")
        stacked = [sem(f"stacked{h}") for h in range(2)]
        gn_stat = sem("gn_stat")
        gn_dev = sem("gn_dev")
        gn_scale = sem("gn_scale")
        acc_init = sem("acc_init")
        x1_init = sem("x1_init")
        xp_ready = sem("xp_ready")
        tapped = sem("tapped")
        x_in = sem("x_in")
        y_out = sem("y_out")

        N_W = 8 + KK
        N_PADS = 10
        x_v = x.rearrange("b h w c -> b (h w) c").rearrange("b (p t) c -> b p t c", t=TT)
        out_v = out.rearrange("b h w c -> b (h w) c").rearrange("b (p t) c -> b p t c", t=TT)
        soft_order = ["sub1", "sum1", "inv1", "mul1", "max0", "sub0", "sum0", "inv0", "mul0", "max1"]
        X0t = X0[:, :].rearrange("c (p t) -> c t p", t=TT)
        ACCf = ACC[:, :, :].rearrange("c h w -> c (h w)")
        ACCt = ACCf.rearrange("c (p t) -> c t p", t=TT)
        X0i = X0[:, :].rearrange("c (h w) -> c h w", w=SIDE)

        def a4(h):
            return att[:, 0:KK * ROWS[h] * WIN].rearrange("r (k i j) -> r k i j", k=KK, j=WIN)

        def soft(i, name):
            return upto(10, i, soft_order.index(name) + 1)

        def use_done(i, kind, which, k):
            return upto(N_USES, i, use_no(kind, which, k) + 1)

        def use_on(kind, which, s1, s2, cv):
            if kind == V and which == 1:
                return s2
            if kind == OUT or (kind in (GA, GB) and which == 2):
                return cv
            return s1

        def until(eng, sm, value):
            if not isinstance(value, int) or value > 0:
                eng.wait_ge(sm, value)

        def skip(eng, sm, n=1):
            eng.drain().then_inc(sm, n)

        def steps(eng, body):
            body(-1, True, False, False)
            body(0, True, True, False)
            with eng.Fori(1, BATCH - 1) as i:
                body(i, True, True, True)
            body(BATCH - 1, False, True, True)
            body(BATCH, False, False, True)

        block = ctx.enter_context(nc.Block())

        @block.sync
        def _(sp):
            for dst, src in ((idn[:, :], ident), (grp[:, :], group), (wv[:, :], W_v), (wo[:, :], W_o),
                             (bo[:, :], b_o.rearrange("(c o) -> c o", o=1)),
                             (tok_out[0:CH, 0:11, :].rearrange("c a b -> c (a b)")[:, 0:KK * QN], W_a)):
                sp.dma_start(dst, src).then_inc(weights_in, 16)
            sp.dma_start(tok_in[0:3 * PN, 0:TAPS, :], select).then_inc(weights_in, 16)
            ba_v = b_a.rearrange("(n q k) -> q n k", n=HEADS, q=KK)
            for q in range(KK):
                sp.dma_start(ba[q * HEADS:(q + 1) * HEADS, :], ba_v[q]).then_inc(weights_in, 16)
            sp.dma_start(wc[:, :], w_conv).then_inc(weights_in, 16)
            sp.sem_inc(y_out, 16)
            sp.wait_ge(weights_up, 2)

            def restack(i, h):
                for p, ready in enumerate((hi_done, mid_done, lo_done)):
                    until(sp, ready, upto(2, i, 1 if h else 2))
                    for q in range(TAPS):
                        sp.dma_start(stack[h][p * PN:(p + 1) * PN, q, :, 0:ROWS[h], :],
                                     parts[p][q * PN:(q + 1) * PN, :, 0:ROWS[h], :]).then_inc(stacked[h], 16)

            def body(i, s1, s2, cv):
                if s1:
                    until(sp, side_full, use_done(i - 1, IN, 0, 6))
                    sp.dma_start(tok_in[:, :, :], x_v[i + 1]).then_inc(x_in, 16)
                if s2:
                    restack(i, 1)
                if s1:
                    restack(i, 0)
                if cv:
                    until(sp, side_read, use_done(i, OUT, 0, 6))
                    sp.dma_start(out_v[i - 1], tok_out[:, :, :]).then_inc(y_out, 16)

            steps(sp, body)
            sp.wait_ge(y_out, 16 * (BATCH + 1))

        @block.gpsimd
        def _(pool):
            nc.gpsimd.memset(half_neg[:, :], -0.5).then_inc(pads_zero, 1)
            nc.gpsimd.memset(eps[:, :], 1e-5).then_inc(pads_zero, 1)
            nc.gpsimd.memset(XP[:, :, :], 0.0).then_inc(pads_zero, 1)
            for h in range(2):
                nc.gpsimd.memset(VAL[h][:, :, :], 0.0).then_inc(pads_zero, 1)
                nc.gpsimd.memset(stack[h][:, :, :, :, :], 0.0).then_inc(pads_zero, 1)
            for p in range(3):
                nc.gpsimd.memset(parts[p][:, :, :, :], 0.0).then_inc(pads_zero, 1)
            pool.wait_ge(pads_zero, N_PADS)

            def pooling(i, h):
                n = 0 if h == 0 else 2
                until(pool, xn_ready, upto(2, i, h + 1))
                until(pool, pool_step, upto(4, i, n))
                r0 = 2 * (HALF if h else 0) - PIX0[h]
                nr = 2 * ROWS[h]
                xv = XN[:, r0:r0 + nr, :].rearrange("c r (w two) -> c r w two", two=2)
                nc.gpsimd.tensor_tensor(pc[:, 0:nr, :], xv[:, :, :, 0], xv[:, :, :, 1],
                                        ALU.add).then_inc(pool_step, 1)
                until(pool, pool_step, upto(4, i, n + 1))
                until(pool, side_full, use_done(i, LOG, 0, KK - 1) if h else use_done(i - 1, LOG, 1, KK - 1))
                pv = pc[:, 0:nr, :].rearrange("c (r two) w -> c r two w", two=2)
                nc.gpsimd.tensor_tensor(pooled[:, 0:ROWS[h], :], pv[:, :, 0, :], pv[:, :, 1, :],
                                        ALU.add).then_inc(pool_step, 1)

            def split(i, h, first):
                n = 1 if first else 2
                av, hi, mid, lo = a4(h), *(p[:, :, 0:ROWS[h], 0:WIN] for p in parts)
                until(pool, hi_done, upto(2, i, n))
                nc.gpsimd.tensor_tensor(av, av, hi, ALU.subtract).then_inc(rest_done, 1)
                until(pool, mid_done, upto(2, i, n))
                nc.gpsimd.tensor_tensor(lo, av, mid, ALU.subtract).then_inc(lo_done, 1)

            def norm_scale(i, g):
                n = 0 if g else 3
                c = slice(g, g + 1)
                until(pool, side_read, use_done(i, GB, 2 if g else 1, 0))
                nc.gpsimd.tensor_tensor(gve[:, c], eps[:, :], gvar[:, c], ALU.subtract).then_inc(gn_scale, 1)
                until(pool, gn_scale, upto(6, i, n + 1))
                nc.gpsimd.tensor_tensor(rstd[:, c], gve[:, c], half_neg[:, :], ALU.pow).then_inc(gn_scale, 1)
                until(pool, gn_scale, upto(6, i, n + 2))
                nc.gpsimd.tensor_tensor(shift[:, c], nmean[:, c], rstd[:, c], ALU.mult).then_inc(gn_scale, 1)

            def body(i, s1, s2, cv):
                if cv:
                    norm_scale(i, 1)
                else:
                    skip(pool, gn_scale, 3)
                if s2:
                    split(i, 1, True)
                else:
                    skip(pool, rest_done)
                    skip(pool, lo_done)
                if s1:
                    norm_scale(i, 0)
                    pooling(i, 0)
                    split(i, 0, False)
                    pooling(i, 1)
                else:
                    skip(pool, gn_scale, 3)

            steps(pool, body)

        @block.scalar
        def _(act):
            act.wait_ge(weights_in, 16 * N_W)
            act.wait_ge(pads_zero, N_PADS)

            def read_use(i, n, kind, which, k):
                bank = side[n % 2]
                until(act, side_full, upto(N_USES, i, n + 1))
                if kind == V:
                    h = which
                    r0, r1 = V_CUTS[h][k], V_CUTS[h][k + 1]
                    if k == 0:
                        until(act, prod_ready, upto(BODY, i, 0 if h else SLOTS))
                    top_row = 1 - h
                    ins = nc.scalar.activation(
                        VAL[h][:, top_row + r0:top_row + r1, 1:1 + SIDE],
                        bank[0:CH, 0:(r1 - r0) * SIDE].rearrange("c (r w) -> c r w", w=SIDE), ACT.Identity)
                elif kind == LOG:
                    h, cols = which, ROWS[which] * WIN
                    if k == 0:
                        until(act, lo_done, upto(2, i, h + 1))
                    ins = nc.scalar.activation(att[:, k * cols:(k + 1) * cols], bank[0:QN, 0:cols],
                                               ACT.Identity, bias=ba[:, k:k + 1])
                elif kind == IN:
                    if k == 0:
                        until(act, x1_init, upto(1, i, 1))
                    ins = nc.scalar.activation(X0t[:, 4 * k:4 * k + 4, :],
                                               bank[0:CH, 0:4 * TP].rearrange("c (t p) -> c t p", t=4), ACT.Identity)
                elif kind == OUT:
                    if k == 0:
                        act.wait_ge(y_out, 16 * i)
                    ins = nc.scalar.activation(tok_out[:, 4 * k:4 * k + 4, :],
                                               bank[0:TP, 0:4 * CH].rearrange("p (t c) -> p t c", t=4), ACT.Identity)
                else:
                    g = which - 1
                    ins = nc.scalar.activation((nmean if kind == GA else gvar)[:, g:g + 1], bank[0:CH, 0:1],
                                               ACT.Identity)
                ins.then_inc(side_read, 1)

            def expo(i, h, first):
                n = 1 if first else 2
                a = att[:, 0:KK * ROWS[h] * WIN]
                until(act, soft_step, soft(i, f"sub{h}"))
                nc.scalar.activation(a, a, ACT.Exp, scale=SCALE).then_inc(exp_done, 1)

            def top_part(i, h, first):
                n = 1 if first else 2
                until(act, soft_step, soft(i, f"mul{h}"))
                if h:
                    until(act, stacked[0], 144 * (i + 1))
                else:
                    until(act, stacked[1], 144 * (i + 1))
                until(act, bcast_full, upto(BODY, i, 0 if h else SLOTS))
                nc.scalar.activation(parts[0][:, :, 0:ROWS[h], 0:WIN], a4(h), ACT.Identity).then_inc(hi_done, 1)

            def mid_part(i, h, first):
                until(act, rest_done, upto(2, i, 1 if first else 2))
                nc.scalar.activation(parts[1][:, :, 0:ROWS[h], 0:WIN], a4(h), ACT.Identity).then_inc(mid_done, 1)

            def normed(i, h):
                if h == 0:
                    until(act, gn_scale, upto(6, i, 6))
                until(act, pool_step, upto(4, i, 2 * h))
                until(act, side_read, use_done(i, V, 1 - h, 3))
                rows = slice(PIX0[h], PIX0[h] + PIXN[h])
                nc.scalar.activation(XN[:, 0:PIXN[h], :], X0i[:, rows, :], ACT.Identity,
                                     bias=shift[:, 0:1], scale=rstd[:, 0:1]).then_inc(xn_ready, 1)

            def start_acc(i):
                until(act, y_added, upto(8, i, 0))
                nc.scalar.activation(ACC[:, :, :], X1[:, :, :], ACT.Identity).then_inc(acc_init, 1)

            def start_x1(i):
                until(act, acc_init, upto(1, i, 1))
                until(act, side_read, use_done(i - 1, IN, 0, 6))
                nc.scalar.activation(X1[:, :, :], X0i, ACT.Identity, bias=bo[:, 0:1]).then_inc(x1_init, 1)

            def rimmed(i):
                until(act, gn_scale, upto(6, i, 3))
                nc.scalar.activation(XP[:, 1:1 + SIDE, 1:1 + SIDE], ACC[:, :, :], ACT.Identity,
                                     bias=shift[:, 1:2], scale=rstd[:, 1:2]).then_inc(xp_ready, 1)

            def body(i, s1, s2, cv):
                more = {2: ("acc", cv), 3: ("exp1", s2), 4: ("x1", s2), 9: ("hi1", s2), 12: ("xp", cv),
                        15: ("mid1", s2), 19: ("xn0", s1), 34: ("exp0", s1), 41: ("hi0", s1),
                        47: ("mid0", s1), 49: ("xn1", s1)}
                for g in range(BODY):
                    for n, (at, kind, which, k) in enumerate(USES):
                        if at == g:
                            if use_on(kind, which, s1, s2, cv):
                                read_use(i, n, kind, which, k)
                            else:
                                skip(act, side_read)
                    if g in more:
                        name, on = more[g]
                        do, sm = {
                            "acc": (lambda: start_acc(i), acc_init), "x1": (lambda: start_x1(i), x1_init),
                            "xp": (lambda: rimmed(i), xp_ready),
                            "exp1": (lambda: expo(i, 1, True), exp_done), "exp0": (lambda: expo(i, 0, False), exp_done),
                            "hi1": (lambda: top_part(i, 1, True), hi_done), "hi0": (lambda: top_part(i, 0, False), hi_done),
                            "mid1": (lambda: mid_part(i, 1, True), mid_done), "mid0": (lambda: mid_part(i, 0, False), mid_done),
                            "xn0": (lambda: normed(i, 0), xn_ready), "xn1": (lambda: normed(i, 1), xn_ready),
                        }[name]
                        if on:
                            do()
                        else:
                            skip(act, sm)

            steps(act, body)

        @block.vector
        def _(dve):
            dve.wait_ge(weights_in, 16 * N_W)
            wa_in = tok_out[0:CH, 0:11, :].rearrange("c a b -> c (a b)")[:, 0:KK * QN]
            nc.vector.tensor_scalar(wa[:, :, :, :], wa_in.rearrange("c (n q k) -> c k q n", n=HEADS, q=KK),
                                    0.25, None, ALU.mult).then_inc(weights_up, 1)
            nc.vector.tensor_copy(sel[:, :, :], tok_in[0:3 * PN, 0:TAPS, :]).then_inc(weights_up, 1)
            nc.vector.tensor_scalar(wc[:, :], wc[:, :], -1.0, 1.0, ALU.max, ALU.min).then_inc(weights_up, 1)
            dve.wait_ge(weights_up, 3)
            nc.vector.tensor_scalar(sg[:, :], wc[:, :], 0.0, None, ALU.is_gt).then_inc(weights_up, 1)
            nc.vector.tensor_scalar(sg2[:, :], wc[:, :], 0.0, None, ALU.is_lt).then_inc(weights_up, 1)
            dve.wait_ge(weights_up, 5)
            nc.vector.tensor_tensor(sg[:, :], sg[:, :], sg2[:, :], ALU.subtract).then_inc(weights_up, 1)
            dve.wait_ge(weights_up, 6)
            nc.vector.tensor_tensor(sg[:, :], sg[:, :], wc[:, :], ALU.subtract).then_inc(weights_up, 1)
            dve.wait_ge(weights_up, 7)
            nc.vector.tensor_tensor(sg[:, :], sg[:, :], wc[:, :], ALU.add).then_inc(weights_up, 1)
            dve.wait_ge(weights_up, 8)
            dve.wait_ge(pads_zero, N_PADS)

            def product(i, g):
                h, s = divmod(g, SLOTS)
                if s == 0:
                    until(dve, side_read, use_done(i, V, 1, 3) if h else use_done(i - 1, V, 0, 3))
                (_, r0, c0, _), (_, r1, c1, _) = TERMS[2 * s:2 * s + 2]
                v0 = VAL[h][:, r0:r0 + 2 * HALF - 1:2, c0:c0 + 2 * WIN - 1:2]
                v = bass.AP(v0.tensor, v0.offset, [v0.ap[0], [(r1 - r0) * PAD_V + c1 - c0, 2], *v0.ap[1:]])
                until(dve, bcast_full, upto(BODY, i, g + 1))
                until(dve, summed, upto(BODY, i, g + 1 - PRODUCTS))
                b = bc[g % 2][0:CH, :, 0:UNIT].rearrange("c a (i j) -> c a i j", j=WIN)
                nc.vector.tensor_tensor(prod[:, g % PRODUCTS, :, :].rearrange("c a (i j) -> c a i j", j=WIN),
                                        b, v, ALU.mult).then_inc(prod_ready, 1)

            def add_class(i, h, c):
                until(dve, summed, upto(BODY, i, h * SLOTS + LAST[c] + 1))
                if h == 0 and c == 0:
                    until(dve, x1_init, upto(1, i, 1))
                pr, pq = CLASSES[c]
                r0 = 2 * HALF * h + pr
                xv = X1[:, r0:r0 + 2 * HALF - 1:2, pq:pq + 2 * WIN - 1:2]
                nc.vector.tensor_tensor(xv, acc[c % 2][0:CH, 0:UNIT].rearrange("c (i j) -> c i j", j=WIN), xv,
                                        ALU.add).then_inc(y_added, 1)

            def soft_max(i, h):
                until(dve, side_read, use_done(i, LOG, h, KK - 1))
                until(dve, soft_step, soft(i, f"max{h}") - 1)
                n = ROWS[h] * WIN
                nc.vector.tensor_reduce(top[:, 0:n], att[:, 0:KK * n].rearrange("r (k n) -> r n k", k=KK), AX.X,
                                        ALU.max).then_inc(soft_step, 1)

            def soft_sub(i, h):
                n = ROWS[h] * WIN
                until(dve, soft_step, soft(i, f"sub{h}") - 1)
                a = att[:, 0:KK * n].rearrange("r (k n) -> r k n", k=KK)
                nc.vector.tensor_tensor(a, a, top[:, 0:n].unsqueeze(1).broadcast_to([QN, KK, n]),
                                        ALU.subtract).then_inc(soft_step, 1)

            def soft_sum(i, h, first):
                n = ROWS[h] * WIN
                until(dve, exp_done, upto(2, i, 1 if first else 2))
                nc.vector.tensor_reduce(top[:, 0:n], att[:, 0:KK * n].rearrange("r (k n) -> r n k", k=KK), AX.X,
                                        ALU.add).then_inc(soft_step, 1)

            def soft_div(i, h):
                n = ROWS[h] * WIN
                a = att[:, 0:KK * n].rearrange("r (k n) -> r k n", k=KK)
                until(dve, soft_step, soft(i, f"sum{h}"))
                nc.vector.reciprocal(top[:, 0:n], top[:, 0:n]).then_inc(soft_step, 1)
                until(dve, soft_step, soft(i, f"inv{h}"))
                nc.vector.tensor_tensor(a, a, top[:, 0:n].unsqueeze(1).broadcast_to([QN, KK, n]),
                                        ALU.mult).then_inc(soft_step, 1)

            def channel_stats(i, g):
                n = 0 if g else 3
                if g:
                    until(dve, acc_init, upto(1, i, 1))
                else:
                    until(dve, side_read, use_done(i, IN, 0, 6))
                src = ACCf if g else X0[:, :]
                for k in range(7):
                    last = nc.vector.bn_stats(stats[:, g, k, :], src[:, CHUNK * k:CHUNK * (k + 1)])
                last.then_inc(gn_stat, 1)

            def channel_means(i, g):
                nc.vector.bn_aggr(mv[:, g, :], stats[:, g, :, :].rearrange("c a b -> c (a b)")).then_inc(gn_stat, 1)

            def group_dev(i, g):
                n = 0 if g else 3
                c = slice(g, g + 1)
                until(dve, side_read, use_done(i, GA, 2 if g else 1, 0))
                until(dve, gn_stat, upto(6, i, n + 2))
                nc.vector.tensor_tensor(dev[:, c], mv[:, g, 0:1], nmean[:, c], ALU.add).then_inc(gn_dev, 1)
                until(dve, gn_dev, upto(2, i, 1 if g else 2))
                nc.vector.scalar_tensor_tensor(dev2[:, c], dev[:, c], dev[:, c], mv[:, g, 1:2], ALU.mult,
                                               ALU.add).then_inc(gn_stat, 1)

            def tap(i, n):
                t, part = divmod(n, 2)
                ty, tx = divmod(t, TAPS)
                r0 = part * (SIDE // 2)
                if n == 0:
                    until(dve, xp_ready, upto(1, i, 1))
                until(dve, tapped, upto(18, i, n - 1))
                a = ACC[:, r0:r0 + SIDE // 2, :]
                nc.vector.scalar_tensor_tensor(a, XP[:, r0 + ty:r0 + ty + SIDE // 2, tx:tx + SIDE], sg[:, t:t + 1], a,
                                               ALU.mult, ALU.add).then_inc(tapped, 1)

            add_at = {min(LAST[c] + LAG + 1, SLOTS - 1): c for c in range(3)}

            def body(i, s1, s2, cv):
                plan = {0: ("sub1", s2), 2: ("stats1", cv), 3: ("mean1", cv), 5: ("sum1", s2), 7: ("div1", s2), 9: ("dev1", cv),
                        15: ("stats0", s1), 16: ("mean0", s1), 17: ("dev0", s1), 31: ("max0", s1), 32: ("sub0", s1),
                        36: ("sum0", s1), 38: ("div0", s1), 63: ("max1", s1)}
                do = {"sub1": lambda: soft_sub(i, 1), "sum1": lambda: soft_sum(i, 1, True), "div1": lambda: soft_div(i, 1),
                      "sub0": lambda: soft_sub(i, 0), "sum0": lambda: soft_sum(i, 0, False), "div0": lambda: soft_div(i, 0),
                      "max0": lambda: soft_max(i, 0), "max1": lambda: soft_max(i, 1),
                      "stats1": lambda: channel_stats(i, 1), "mean1": lambda: channel_means(i, 1), "mean0": lambda: channel_means(i, 0), "dev1": lambda: group_dev(i, 1),
                      "stats0": lambda: channel_stats(i, 0), "dev0": lambda: group_dev(i, 0)}
                for g in range(BODY):
                    h, s = divmod(g, SLOTS)
                    if g == 3 and cv:
                        until(dve, gn_stat, upto(6, i, 1))
                    if g == 16 and s1:
                        until(dve, gn_stat, upto(6, i, 4))
                    if s2:
                        product(i, g)
                    else:
                        if s == 0 and s1:
                            skip(dve, prod_ready, SLOTS)
                            skip(dve, y_added, 4)
                    if s2 and s in add_at:
                        add_class(i, h, add_at[s])
                    if s == 2 and (s2 if h else cv):
                        add_class(i if h else i - 1, 1 - h, 3)
                    if g in plan:
                        name, on = plan[g]
                        if on:
                            do[name]()
                        elif name.startswith("stats") or name.startswith("mean"):
                            skip(dve, gn_stat)
                        elif name.startswith("dev"):
                            skip(dve, gn_stat)
                            skip(dve, gn_dev)
                        else:
                            skip(dve, soft_step, 2 if name.startswith("div") else 1)
                    for n, at in enumerate(TAP_SLOTS):
                        if at == g:
                            if cv:
                                tap(i, n)
                            else:
                                skip(dve, tapped)

            steps(dve, body)

        @block.tensor
        def _(pe):
            pe.wait_ge(weights_in, 16 * N_W)
            pe.wait_ge(weights_up, 2)
            pe.wait_ge(pads_zero, N_PADS)

            def fill_use(i, n, kind, which, k):
                bank = side[n % 2]
                until(pe, side_read, upto(N_USES, i, n - 1))
                if kind == V:
                    h = which
                    r0, r1 = V_CUTS[h][k], V_CUTS[h][k + 1]
                    if k == 0:
                        until(pe, xn_ready, upto(2, i, 0) if h else upto(2, i, 1))
                    last = nc.tensor.matmul(bank[0:CH, 0:(r1 - r0) * SIDE], wv[:, :], XN[:, r0:r1, :],
                                            start=True, stop=True)
                elif kind == LOG:
                    h = which
                    if k == 0:
                        until(pe, pool_step, upto(4, i, 2 * h + 2))
                    last = nc.tensor.matmul(bank[0:QN, 0:ROWS[h] * WIN], wa[:, k, :, :],
                                            pooled[:, 0:ROWS[h], :], start=True, stop=True)
                elif kind == IN:
                    if k == 0:
                        until(pe, x_in, 16 * (i + 2))
                    for t in range(4):
                        last = nc.tensor.transpose(bank[0:CH, t * TP:(t + 1) * TP], tok_in[:, 4 * k + t, :], idn[:, :])
                elif kind == OUT:
                    if k == 0:
                        until(pe, tapped, upto(18, i, 18))
                    for t in range(4):
                        last = nc.tensor.transpose(bank[0:TP, t * CH:(t + 1) * CH], ACCt[:, 4 * k + t, :],
                                                   idn[0:CH, 0:CH])
                else:
                    g = which - 1
                    until(pe, gn_stat, upto(6, i, (0 if g else 3) + (2 if kind == GA else 3)))
                    src = mv[:, g, 0:1] if kind == GA else dev2[:, g:g + 1]
                    last = nc.tensor.matmul(bank[0:CH, 0:1], grp[:, :], src, start=True, stop=True)
                last.then_inc(side_full, 1)

            def broadcast(i, g):
                h, s = divmod(g, SLOTS)
                if s == 0:
                    until(pe, stacked[h], 144 * (i + 1))
                until(pe, prod_ready, upto(BODY, i, g - 1))
                for a in range(2):
                    _, _, _, who = TERMS[2 * s + a]
                    for n, ((si, qi, ki), (sj, qj, kj)) in enumerate(who):
                        last = nc.tensor.matmul(
                            bc[g % 2][0:CH, a, 0:UNIT], sel[:, qj, :],
                            stack[h][:, qi, ki * TAPS + kj, si:si + HALF, sj:sj + WIN],
                            start=(n == 0), stop=(n == len(who) - 1))
                last.then_inc(bcast_full, 1)

            def add_up(i, g):
                h, s = divmod(g, SLOTS)
                until(pe, prod_ready, upto(BODY, i, g + 1))
                for a in range(2):
                    t = 2 * s + a
                    c = TERMS[t][0]
                    first = t == 0 or TERMS[t - 1][0] != c
                    if first:
                        until(pe, y_added, upto(8, i, 4 * h + c - 1))
                    last = nc.tensor.matmul(acc[c % 2][0:CH, 0:UNIT], wo[:, :], prod[:, g % PRODUCTS, a, :],
                                            start=first, stop=(t == len(TERMS) - 1 or TERMS[t + 1][0] != c))
                last.then_inc(summed, 1)

            def body(i, s1, s2, cv):
                for g in range(BODY):
                    h, s = divmod(g, SLOTS)
                    if s2:
                        broadcast(i, g)
                        if g >= LAG:
                            add_up(i, g - LAG)
                    elif s1 and s == 0:
                        skip(pe, bcast_full, SLOTS)
                        skip(pe, summed, SLOTS)
                    if g < LAG and cv:
                        add_up(i - 1, BODY + g - LAG)
                    for n, (at, kind, which, k) in enumerate(USES):
                        if at == g:
                            if use_on(kind, which, s1, s2, cv):
                                fill_use(i, n, kind, which, k)
                            else:
                                skip(pe, side_full)

            steps(pe, body)


_INS = ["x", "L0_conv_W_v", "L0_conv_W_a", "L0_conv_b_a", "L0_conv_W_o", "L0_conv_b_o", "L1_conv_w"]


def kernel(**inputs):
    import numpy as np
    from concourse import bacc
    from concourse.bass_utils import run_bass_kernel_spmd

    ident = np.eye(TP, dtype=np.float32)
    chan = np.arange(CH)
    group = np.where(chan[:, None] // GROUP == chan[None, :] // GROUP, np.float32(-1.0 / GROUP), np.float32(0.0))
    row = np.arange(3 * PN)
    select = ((row[:, None, None] // HEADS % TAPS == np.arange(TAPS)[None, :, None])
              & (row[:, None, None] % HEADS == chan[None, None, :] // DIM)).astype(np.float32)

    nc = bacc.Bacc("TRN2", target_bir_lowering=False, num_devices=1)
    arrays, args = {}, []
    for name in _INS:
        arrays["in_" + name] = np.ascontiguousarray(inputs[name])
    arrays["in_L1_conv_w"] = np.ascontiguousarray(np.asarray(inputs["L1_conv_w"]).reshape(KK, CH).T)
    arrays["ident"], arrays["group"], arrays["select"] = ident, group, select
    for name, a in arrays.items():
        args.append(nc.dram_tensor(name, a.shape, mybir.dt.from_np(a.dtype), kind="ExternalInput").ap())
    args.append(nc.dram_tensor("out", (BATCH, SIDE, SIDE, CH), mybir.dt.float32, kind="ExternalOutput").ap())
    build_program(nc, *args)
    r = run_bass_kernel_spmd(nc, [arrays], core_ids=[0])
    return r.results[0]["out"]
```

```python
import concourse.bass as bass
from concourse import mybir
from contextlib import ExitStack

BATCH, SIDE, CH = 32, 56, 96
HEADS, DIM, TAPS = 12, 8, 3
GROUP = 3
WIN = SIDE // 2
GRID = WIN + 1
PIX = SIDE * SIDE
PAD_P = SIDE + 2
PAD_V = SIDE + 3
TP, TT = 112, PIX // 112
HALF = WIN // 2
UNIT = HALF * WIN
ROWS = (HALF + 1, HALF)
PIX0 = (0, SIDE // 2 - 1)
PIXN = (SIDE // 2 + 2, SIDE // 2 + 1)
V_ROWS = 2 * (HALF - 1) + 5
KK = TAPS * TAPS
QN = KK * HEADS
PN = TAPS * HEADS
CHUNK = 448
SCALE = float(DIM) ** -0.5

AXIS = {
    0: [(0, [(0, 1, 0)]), (1, [(0, 1, 1)]), (2, [(0, 1, 2)])],
    1: [(0, [(0, 2, 0)]), (1, [(0, 2, 1)]), (2, [(0, 2, 2), (1, 0, 0)]), (3, [(1, 0, 1)]), (4, [(1, 0, 2)])],
}
CLASSES = [(1, 1), (1, 0), (0, 1), (0, 0)]
TERMS = [(c, rv, cv, [(r, cols[0], TAPS if len(cols) == 2 else cols[0][1]) for r in rows])
         for c, (pr, pc) in enumerate(CLASSES) for rv, rows in AXIS[pr] for cv, cols in AXIS[pc]]
SLOTS = len(TERMS) // 2
NOT_PRE = (0, 4, 14, 24, 30, 31)
LAST = [max(n for n, t in enumerate(TERMS) if t[0] == c) // 2 for c in range(4)]
BODY = 2 * SLOTS
LAG = 3
PRODUCTS = 4
V_CUTS = ((0, 8, 16, 23, 30), (0, 8, 15, 22, 29))

PARTS = 2
STACKED = PARTS * (TAPS + 1) * HEADS
SELS = TAPS + 1
PART_UP = 4096.0
PRE = [s for s in range(SLOTS) if TERMS[2 * s][0] == TERMS[2 * s + 1][0] and s not in NOT_PRE]
V, LOG, IN, OUT, GA, GB = "values", "logits", "in", "out", "mean", "var"
USES = sorted(
    [(0 + k, V, 1, k) for k in range(4)] + [(9, GA, 2, 0), (11, GB, 2, 0)]
    + [(7 + k, IN, 0, k) for k in range(7)] + [(17, GA, 1, 0), (18, GB, 1, 0)]
    + [(23 + k, LOG, 0, k) for k in range(KK)]
    + [(SLOTS + k, V, 0, k) for k in range(4)]
    + [(57 + k, OUT, 0, k) for k in range(7)]
    + [(SLOTS + 23 + k, LOG, 1, k) for k in range(KK)], key=lambda u: u[0])
N_USES = len(USES)
assert N_USES % 2 == 0
MAX, SUB, SUM, INV = "max", "subtract", "sum", "invert"
SOFT = sorted([(base + at, what, h, n) for base, h in ((0, 1), (SLOTS, 0)) for what, ats in (
    (MAX, (0, 1, 2, 3)), (SUB, (4, 5, 6)), (SUM, (8, 9, 10, 11)), (INV, (10, 11, 12, 13)))
    for n, at in enumerate(ats)], key=lambda p: p[0])
MUL, LOW = "multiply", "low"
FINE = [(MUL, 0), (MUL, 1), (MUL, 2), (MUL, 3), (MUL, 4), (MUL, 5), (LOW, 0), (LOW, 1), (LOW, 2),
        (MUL, 6), (MUL, 7), (MUL, 8), (LOW, 3), (LOW, 4), (LOW, 5), (LOW, 6), (LOW, 7), (LOW, 8)]
FINE_AT = [14 + n * 13 // 18 for n in range(18)]


def soft_no(what, h, n):
    return next(m for m, p in enumerate(SOFT) if p[1:] == (what, h, n)) + 1


def pre_no(g):
    h, s = divmod(g, SLOTS)
    return h * len(PRE) + PRE.index(s) + 1


def use_no(kind, which, k):
    return next(n for n, u in enumerate(USES) if u[1:] == (kind, which, k))


TAP_SLOTS = sorted(list(range(13, 32)) + [34, 38, 42, 45] + list(range(46, 57)) + [50, 54])
assert len(TAP_SLOTS) == 36


def upto(per_body, i, n):
    return (i + 1) * per_body + n


def build_program(nc, x, W_v, W_a, b_a, W_o, b_o, w_conv, ident, group, select, out):
    F32, F16 = mybir.dt.float32, mybir.dt.float16
    ALU, ACT, AX = mybir.AluOpType, mybir.ActivationFunctionType, mybir.AxisListType
    ctx = ExitStack()
    with ctx:
        def sb(name, shape, dt=F32):
            return ctx.enter_context(nc.sbuf_tensor(name, shape, dt))

        def sem(name):
            return ctx.enter_context(nc.semaphore(name))

        idn = sb("idn", [TP, TP])
        grp = sb("grp", [CH, CH])
        sel = sb("sel", [STACKED, SELS, CH], F16)
        wv = sb("wv", [CH, CH])
        wo = sb("wo", [CH, CH])
        wa = sb("wa", [CH, KK, KK, HEADS])
        ba = sb("ba", [QN, KK])
        bo = sb("bo", [CH, 1])
        wc = sb("wc", [CH, KK])
        sg = sb("sg", [CH, KK])
        sg2 = sb("sg2", [CH, KK])
        half_neg = sb("half_neg", [CH, 1])
        eps = sb("eps", [CH, 1])
        tok_in = sb("tok_in", [TP, TT, CH])
        tok_out = sb("tok_out", [TP, TT, CH])
        X0 = sb("X0", [CH, PIX])
        XN = sb("XN", [CH, PIXN[0], SIDE])
        X1 = sb("X1", [CH, SIDE, SIDE])
        ACC = sb("ACC", [CH, SIDE, SIDE])
        XP = sb("XP", [CH, PAD_P, PAD_P])
        VAL = [sb(f"VAL{h}", [CH, V_ROWS, PAD_V]) for h in range(2)]
        pc = sb("pc", [CH, PIXN[0], WIN])
        pooled = sb("pooled", [CH, ROWS[0], WIN])
        att = sb("att", [QN, KK, ROWS[0] * WIN])
        top = sb("top", [QN, ROWS[0] * WIN])
        parts = [sb(f"part{p}", [QN, KK, ROWS[0], GRID], F16) for p in range(PARTS)]
        stack = [sb(f"stack{h}", [STACKED, TAPS, KK, HALF + 1, GRID], F16) for h in range(2)]
        prod = sb("prod", [CH, PRODUCTS, 2, UNIT])
        stats = sb("stats", [CH, 2, 7, 6])
        mv = sb("mv", [CH, 2, 2])
        nmean = sb("nmean", [CH, 2])
        dev = sb("dev", [CH, 2])
        dev2 = sb("dev2", [CH, 2])
        gvar = sb("gvar", [CH, 2])
        gve = sb("gve", [CH, 2])
        rstd = sb("rstd", [CH, 2])
        shift = sb("shift", [CH, 2])

        bc = [ctx.enter_context(nc.psum_tensor(f"bc{b}", [128, 2, 512], F32)) for b in range(2)]
        acc = [ctx.enter_context(nc.psum_tensor(f"acc{b}", [128, 512], F32)) for b in range(2)]
        side = [ctx.enter_context(nc.psum_tensor(f"side{b}", [128, 512], F32)) for b in range(2)]

        weights_in = sem("weights_in")
        weights_up = sem("weights_up")
        pads_zero = sem("pads_zero")
        bcast_full = sem("bcast_full")
        prod_ready = sem("prod_ready")
        summed = sem("summed")
        y_added = sem("y_added")
        side_full = sem("side_full")
        side_read = sem("side_read")
        xn_ready = sem("xn_ready")
        pool_step = sem("pool_step")
        soft_step = sem("soft_step")
        exp_done = sem("exp_done")
        inv_up = sem("inv_up")
        scaled = sem("scaled")
        hi_done = sem("hi_done")
        lo_done = sem("lo_done")
        pre_added = sem("pre_added")
        stacked = [sem(f"stacked{h}") for h in range(2)]
        gn_chunk = sem("gn_chunk")
        gn_stat = sem("gn_stat")
        gn_dev = sem("gn_dev")
        gn_scale = sem("gn_scale")
        acc_init = sem("acc_init")
        x1_init = sem("x1_init")
        xp_ready = sem("xp_ready")
        tapped = sem("tapped")
        x_in = sem("x_in")
        y_out = sem("y_out")

        N_W = 8 + KK
        N_PADS = 9
        RESTACK = 16 * 4 * PARTS * TAPS // 2
        x_v = x.rearrange("b h w c -> b (h w) c").rearrange("b (p t) c -> b p t c", t=TT)
        out_v = out.rearrange("b h w c -> b (h w) c").rearrange("b (p t) c -> b p t c", t=TT)
        X0t = X0[:, :].rearrange("c (p t) -> c t p", t=TT)
        ACCf = ACC[:, :, :].rearrange("c h w -> c (h w)")
        ACCt = ACCf.rearrange("c (p t) -> c t p", t=TT)
        X0i = X0[:, :].rearrange("c (h w) -> c h w", w=SIDE)

        def a4(h):
            return att[:, :, 0:ROWS[h] * WIN].rearrange("r k (i j) -> r k i j", j=WIN)

        def soft_done(i, what, h, n):
            return upto(len(SOFT), i, soft_no(what, h, n))

        def turn(h):
            return 0 if h else 1

        def use_done(i, kind, which, k):
            return upto(N_USES, i, use_no(kind, which, k) + 1)

        def use_on(kind, which, s1, s2, cv):
            if kind == V and which == 1:
                return s2
            if kind == OUT or (kind in (GA, GB) and which == 2):
                return cv
            return s1

        def until(eng, sm, value):
            if not isinstance(value, int) or value > 0:
                eng.wait_ge(sm, value)

        def skip(eng, sm, n=1):
            eng.drain().then_inc(sm, n)

        def steps(eng, body):
            body(-1, True, False, False)
            body(0, True, True, False)
            with eng.Fori(1, BATCH - 1) as i:
                body(i, True, True, True)
            body(BATCH - 1, False, True, True)
            body(BATCH, False, False, True)

        block = ctx.enter_context(nc.Block())

        @block.sync
        def _(sp):
            for dst, src in ((idn[:, :], ident), (grp[:, :], group), (wv[:, :], W_v), (wo[:, :], W_o),
                             (bo[:, :], b_o.rearrange("(c o) -> c o", o=1)),
                             (tok_out[0:CH, 0:11, :].rearrange("c a b -> c (a b)")[:, 0:KK * QN], W_a)):
                sp.dma_start(dst, src).then_inc(weights_in, 16)
            sp.dma_start(tok_in[0:STACKED, 0:SELS, :], select).then_inc(weights_in, 16)
            ba_v = b_a.rearrange("(n q k) -> q n k", n=HEADS, q=KK)
            for q in range(KK):
                sp.dma_start(ba[q * HEADS:(q + 1) * HEADS, :], ba_v[q]).then_inc(weights_in, 16)
            sp.dma_start(wc[:, :], w_conv).then_inc(weights_in, 16)
            sp.sem_inc(y_out, 16)
            sp.wait_ge(weights_up, 2)

            def restack(i, h):
                for p, (ready, n) in enumerate(((hi_done, 3), (lo_done, KK))):
                    until(sp, ready, upto(2 * n, i, n * (turn(h) + 1)))
                    for q in range(TAPS):
                        sp.dma_start(stack[h][p * PN:(p + 1) * PN, q, :, 0:ROWS[h], :],
                                     parts[p][q * PN:(q + 1) * PN, :, 0:ROWS[h], :]).then_inc(stacked[h], 16)
                        row = PARTS * PN + p * HEADS
                        n = ROWS[h] * GRID - 1
                        sp.dma_start(
                            stack[h][row:row + HEADS, q].rearrange("r (a b) i j -> r a b (i j)", b=TAPS)[:, :, 2, 0:n],
                            parts[p][q * PN:q * PN + HEADS].rearrange("r (a b) i j -> r a b (i j)", b=TAPS)[:, :, 0, 1:n + 1],
                        ).then_inc(stacked[h], 16)

            def body(i, s1, s2, cv):
                if s1:
                    until(sp, side_full, use_done(i - 1, IN, 0, 6))
                    sp.dma_start(tok_in[:, :, :], x_v[i + 1]).then_inc(x_in, 16)
                if s2:
                    restack(i, 1)
                if s1:
                    restack(i, 0)
                if cv:
                    until(sp, side_read, use_done(i, OUT, 0, 6))
                    sp.dma_start(out_v[i - 1], tok_out[:, :, :]).then_inc(y_out, 16)

            steps(sp, body)
            sp.wait_ge(y_out, 16 * (BATCH + 1))

        @block.gpsimd
        def _(pool):
            nc.gpsimd.memset(half_neg[:, :], -0.5).then_inc(pads_zero, 1)
            nc.gpsimd.memset(eps[:, :], 1e-5).then_inc(pads_zero, 1)
            nc.gpsimd.memset(XP[:, :, :], 0.0).then_inc(pads_zero, 1)
            for h in range(2):
                nc.gpsimd.memset(VAL[h][:, :, :], 0.0).then_inc(pads_zero, 1)
                nc.gpsimd.memset(stack[h][:, :, :, :, :], 0.0).then_inc(pads_zero, 1)
            for p in range(PARTS):
                nc.gpsimd.memset(parts[p][:, :, :, :], 0.0).then_inc(pads_zero, 1)
            pool.wait_ge(pads_zero, N_PADS)

            def pooling(i, h):
                n = 0 if h == 0 else 2
                until(pool, xn_ready, upto(2, i, h + 1))
                until(pool, pool_step, upto(4, i, n))
                r0 = 2 * (HALF if h else 0) - PIX0[h]
                nr = 2 * ROWS[h]
                xv = XN[:, r0:r0 + nr, :].rearrange("c r (w two) -> c r w two", two=2)
                nc.gpsimd.tensor_tensor(pc[:, 0:nr, :], xv[:, :, :, 0], xv[:, :, :, 1],
                                        ALU.add).then_inc(pool_step, 1)
                until(pool, pool_step, upto(4, i, n + 1))
                until(pool, side_full, use_done(i, LOG, 0, KK - 1) if h else use_done(i - 1, LOG, 1, KK - 1))
                pv = pc[:, 0:nr, :].rearrange("c (r two) w -> c r two w", two=2)
                nc.gpsimd.tensor_tensor(pooled[:, 0:ROWS[h], :], pv[:, :, 0, :], pv[:, :, 1, :],
                                        ALU.add).then_inc(pool_step, 1)

            def fine(i, h, what, k):
                n = ROWS[h] * WIN
                m = KK * turn(h)
                if what == MUL:
                    until(pool, inv_up, upto(2, i, turn(h) + 1))
                    a = att[:, k, 0:n]
                    nc.gpsimd.tensor_tensor(a, a, top[:, 0:n], ALU.mult).then_inc(scaled, 1)
                else:
                    until(pool, hi_done, upto(6, i, 3 * turn(h) + k // 3 + 1))
                    if k == 0:
                        until(pool, stacked[1 - h], RESTACK * (i + 1))
                    nc.gpsimd.tensor_tensor(parts[1][:, k, 0:ROWS[h], 0:WIN], a4(h)[:, k], parts[0][:, k, 0:ROWS[h], 0:WIN],
                                            ALU.subtract).then_inc(lo_done, 1)

            def pre_add(i, g):
                until(pool, prod_ready, upto(BODY, i, g + 1))
                p = prod[:, g % PRODUCTS, :, :]
                nc.gpsimd.tensor_tensor(p[:, 0, :], p[:, 0, :], p[:, 1, :], ALU.add).then_inc(pre_added, 1)

            def norm_scale(i, g):
                n = 0 if g else 3
                c = slice(g, g + 1)
                until(pool, side_read, use_done(i, GB, 2 if g else 1, 0))
                nc.gpsimd.tensor_tensor(gve[:, c], eps[:, :], gvar[:, c], ALU.subtract).then_inc(gn_scale, 1)
                until(pool, gn_scale, upto(6, i, n + 1))
                nc.gpsimd.tensor_tensor(rstd[:, c], gve[:, c], half_neg[:, :], ALU.pow).then_inc(gn_scale, 1)
                until(pool, gn_scale, upto(6, i, n + 2))
                nc.gpsimd.tensor_tensor(shift[:, c], nmean[:, c], rstd[:, c], ALU.mult).then_inc(gn_scale, 1)

            def body(i, s1, s2, cv):
                for g in range(BODY):
                    h, s = divmod(g, SLOTS)
                    on = s1 if h else s2
                    for n, at in enumerate(FINE_AT):
                        if at == s:
                            if on:
                                fine(i, 1 - h, *FINE[n])
                            else:
                                skip(pool, scaled if FINE[n][0] == MUL else lo_done)
                    for at, do, sm, n, which in ((11, lambda: norm_scale(i, 1), gn_scale, 3, cv),
                                                 (18, lambda: norm_scale(i, 0), gn_scale, 3, s1),
                                                 (20, lambda: pooling(i, 0), pool_step, 2, s1),
                                                 (51, lambda: pooling(i, 1), pool_step, 2, s1)):
                        if at == g:
                            if which:
                                do()
                            else:
                                skip(pool, sm, n)
                    if s in PRE:
                        if s2:
                            pre_add(i, g)
                        elif s == PRE[0]:
                            skip(pool, pre_added, len(PRE))

            steps(pool, body)

        @block.scalar
        def _(act):
            act.wait_ge(weights_in, 16 * N_W)
            act.wait_ge(pads_zero, N_PADS)

            def read_use(i, n, kind, which, k):
                bank = side[n % 2]
                until(act, side_full, upto(N_USES, i, n + 1))
                if kind == V:
                    h = which
                    r0, r1 = V_CUTS[h][k], V_CUTS[h][k + 1]
                    if k == 0:
                        until(act, prod_ready, upto(BODY, i, 0 if h else SLOTS))
                    top_row = 1 - h
                    ins = nc.scalar.activation(
                        VAL[h][:, top_row + r0:top_row + r1, 1:1 + SIDE],
                        bank[0:CH, 0:(r1 - r0) * SIDE].rearrange("c (r w) -> c r w", w=SIDE), ACT.Identity)
                elif kind == LOG:
                    h, cols = which, ROWS[which] * WIN
                    until(act, lo_done, upto(2 * KK, i, KK * h + k + 1))
                    ins = nc.scalar.activation(att[:, k, 0:cols], bank[0:QN, 0:cols],
                                               ACT.Identity, bias=ba[:, k:k + 1])
                elif kind == IN:
                    if k == 0:
                        until(act, x1_init, upto(1, i, 1))
                    ins = nc.scalar.activation(X0t[:, 4 * k:4 * k + 4, :],
                                               bank[0:CH, 0:4 * TP].rearrange("c (t p) -> c t p", t=4), ACT.Identity)
                elif kind == OUT:
                    if k == 0:
                        act.wait_ge(y_out, 16 * i)
                    ins = nc.scalar.activation(tok_out[:, 4 * k:4 * k + 4, :],
                                               bank[0:TP, 0:4 * CH].rearrange("p (t c) -> p t c", t=4), ACT.Identity)
                else:
                    g = which - 1
                    ins = nc.scalar.activation((nmean if kind == GA else gvar)[:, g:g + 1], bank[0:CH, 0:1],
                                               ACT.Identity)
                ins.then_inc(side_read, 1)

            def expo(i, h, n):
                a = att[:, 3 * n:3 * n + 3, 0:ROWS[h] * WIN]
                until(act, soft_step, soft_done(i, SUB, h, n))
                nc.scalar.activation(a, a, ACT.Exp, scale=SCALE).then_inc(exp_done, 1)

            def scale_up(i, h, n):
                until(act, soft_step, soft_done(i, INV, h, 3))
                t = top[:, 0:ROWS[h] * WIN]
                nc.scalar.activation(t, t, ACT.Identity, scale=PART_UP).then_inc(inv_up, 1)

            def first_part(i, h, n):
                until(act, scaled, upto(2 * KK, i, KK * turn(h) + 3 * n + 3))
                if n == 0:
                    until(act, stacked[1 - h], RESTACK * (i + 1))
                    until(act, bcast_full, upto(BODY, i, 0 if h else SLOTS))
                nc.scalar.activation(parts[0][:, 3 * n:3 * n + 3, 0:ROWS[h], 0:WIN], a4(h)[:, 3 * n:3 * n + 3],
                                     ACT.Identity).then_inc(hi_done, 1)

            def normed(i, h):
                if h == 0:
                    until(act, gn_scale, upto(6, i, 6))
                until(act, pool_step, upto(4, i, 2 * h))
                until(act, side_read, use_done(i, V, 1 - h, 3))
                rows = slice(PIX0[h], PIX0[h] + PIXN[h])
                nc.scalar.activation(XN[:, 0:PIXN[h], :], X0i[:, rows, :], ACT.Identity,
                                     bias=shift[:, 0:1], scale=rstd[:, 0:1]).then_inc(xn_ready, 1)

            def start_acc(i):
                until(act, y_added, upto(8, i, 0))
                nc.scalar.activation(ACC[:, :, :], X1[:, :, :], ACT.Identity).then_inc(acc_init, 1)

            def start_x1(i):
                until(act, acc_init, upto(1, i, 1))
                until(act, side_read, use_done(i - 1, IN, 0, 6))
                nc.scalar.activation(X1[:, :, :], X0i, ACT.Identity, bias=bo[:, 0:1]).then_inc(x1_init, 1)

            def rimmed(i):
                until(act, gn_scale, upto(6, i, 3))
                nc.scalar.activation(XP[:, 1:1 + SIDE, 1:1 + SIDE], ACC[:, :, :], ACT.Identity,
                                     bias=shift[:, 1:2], scale=rstd[:, 1:2]).then_inc(xp_ready, 1)

            def body(i, s1, s2, cv):
                more = [(3, start_acc, (i,), acc_init, cv), (4, start_x1, (i,), x1_init, s2),
                        (12, rimmed, (i,), xp_ready, cv), (19, normed, (i, 0), xn_ready, s1),
                        (50, normed, (i, 1), xn_ready, s1)]
                for base, h, on in ((0, 1, s2), (SLOTS, 0, s1)):
                    more += [(base + 4 + n, expo, (i, h, n), exp_done, on) for n in range(3)]
                    more += [(base + 13, scale_up, (i, h, 0), inv_up, on)]
                    more += [(base + at, first_part, (i, h, n), hi_done, on) for n, at in enumerate((16, 18, 22))]
                for g in range(BODY):
                    for n, (at, kind, which, k) in enumerate(USES):
                        if at == g:
                            if use_on(kind, which, s1, s2, cv):
                                read_use(i, n, kind, which, k)
                            else:
                                skip(act, side_read)
                    for at, do, what, sm, on in more:
                        if at == g:
                            if on:
                                do(*what)
                            else:
                                skip(act, sm)

            steps(act, body)

        @block.vector
        def _(dve):
            dve.wait_ge(weights_in, 16 * N_W)
            wa_in = tok_out[0:CH, 0:11, :].rearrange("c a b -> c (a b)")[:, 0:KK * QN]
            nc.vector.tensor_scalar(wa[:, :, :, :], wa_in.rearrange("c (n q k) -> c k q n", n=HEADS, q=KK),
                                    0.25, None, ALU.mult).then_inc(weights_up, 1)
            nc.vector.tensor_copy(sel[:, :, :], tok_in[0:STACKED, 0:SELS, :]).then_inc(weights_up, 1)
            nc.vector.tensor_scalar(wc[:, :], wc[:, :], -1.0, 1.0, ALU.max, ALU.min).then_inc(weights_up, 1)
            dve.wait_ge(weights_up, 3)
            nc.vector.tensor_scalar(sg[:, :], wc[:, :], 0.0, None, ALU.is_gt).then_inc(weights_up, 1)
            nc.vector.tensor_scalar(sg2[:, :], wc[:, :], 0.0, None, ALU.is_lt).then_inc(weights_up, 1)
            dve.wait_ge(weights_up, 5)
            nc.vector.tensor_tensor(sg[:, :], sg[:, :], sg2[:, :], ALU.subtract).then_inc(weights_up, 1)
            dve.wait_ge(weights_up, 6)
            nc.vector.tensor_tensor(sg[:, :], sg[:, :], wc[:, :], ALU.subtract).then_inc(weights_up, 1)
            dve.wait_ge(weights_up, 7)
            nc.vector.tensor_tensor(sg[:, :], sg[:, :], wc[:, :], ALU.add).then_inc(weights_up, 1)
            dve.wait_ge(weights_up, 8)
            dve.wait_ge(pads_zero, N_PADS)

            def product(i, g):
                h, s = divmod(g, SLOTS)
                if s == 0:
                    until(dve, side_read, use_done(i, V, 1, 3) if h else use_done(i - 1, V, 0, 3))
                (_, r0, c0, _), (_, r1, c1, _) = TERMS[2 * s:2 * s + 2]
                v0 = VAL[h][:, r0:r0 + 2 * HALF - 1:2, c0:c0 + 2 * WIN - 1:2]
                v = bass.AP(v0.tensor, v0.offset, [v0.ap[0], [(r1 - r0) * PAD_V + c1 - c0, 2], *v0.ap[1:]])
                until(dve, bcast_full, upto(BODY, i, g + 1))
                until(dve, summed, upto(BODY, i, g + 1 - PRODUCTS))
                b = bc[g % 2][0:CH, :, 0:UNIT].rearrange("c a (i j) -> c a i j", j=WIN)
                nc.vector.tensor_tensor(prod[:, g % PRODUCTS, :, :].rearrange("c a (i j) -> c a i j", j=WIN),
                                        b, v, ALU.mult).then_inc(prod_ready, 1)

            def add_class(i, h, c):
                until(dve, summed, upto(BODY, i, h * SLOTS + LAST[c] + 1))
                if h == 0 and c == 0:
                    until(dve, x1_init, upto(1, i, 1))
                pr, pq = CLASSES[c]
                r0 = 2 * HALF * h + pr
                xv = X1[:, r0:r0 + 2 * HALF - 1:2, pq:pq + 2 * WIN - 1:2]
                nc.vector.tensor_tensor(xv, acc[c % 2][0:CH, 0:UNIT].rearrange("c (i j) -> c i j", j=WIN), xv,
                                        ALU.add).then_inc(y_added, 1)

            def soft(i, what, h, n):
                w = ROWS[h] * WIN
                c = slice(n * w // 4, (n + 1) * w // 4)
                by_key = att[:, :, 0:w]
                if what == MAX:
                    if n == 0:
                        until(dve, side_read, use_done(i, LOG, 0, KK - 1) if h == 0 else use_done(i - 1, LOG, 1, KK - 1))
                        until(dve, scaled, upto(2 * KK, i, 0 if h else KK))
                    ins = nc.vector.tensor_reduce(top[:, c], by_key.rearrange("r k n -> r n k")[:, c, :], AX.X, ALU.max)
                elif what == SUB:
                    if n == 0:
                        until(dve, soft_step, soft_done(i, MAX, h, 3))
                    a = by_key[:, 3 * n:3 * n + 3, :]
                    ins = nc.vector.tensor_tensor(a, a, top[:, 0:w].unsqueeze(1).broadcast_to([QN, 3, w]), ALU.subtract)
                elif what == SUM:
                    if n == 0:
                        until(dve, exp_done, upto(6, i, 3 * turn(h) + 3))
                    ins = nc.vector.tensor_reduce(top[:, c], by_key.rearrange("r k n -> r n k")[:, c, :], AX.X, ALU.add)
                else:
                    until(dve, soft_step, soft_done(i, SUM, h, n))
                    ins = nc.vector.reciprocal(top[:, c], top[:, c])
                ins.then_inc(soft_step, 1)

            def channel_stats(i, g, k):
                if g:
                    until(dve, acc_init, upto(1, i, 1))
                else:
                    until(dve, side_read, use_done(i, IN, 0, 6))
                src = ACCf if g else X0[:, :]
                nc.vector.bn_stats(stats[:, g, k, :], src[:, CHUNK * k:CHUNK * (k + 1)]).then_inc(gn_chunk, 1)

            def channel_means(i, g):
                nc.vector.bn_aggr(mv[:, g, :], stats[:, g, :, :].rearrange("c a b -> c (a b)")).then_inc(gn_stat, 1)

            def group_dev(i, g):
                n = 0 if g else 2
                c = slice(g, g + 1)
                until(dve, side_read, use_done(i, GA, 2 if g else 1, 0))
                until(dve, gn_stat, upto(4, i, n + 1))
                nc.vector.tensor_tensor(dev[:, c], mv[:, g, 0:1], nmean[:, c], ALU.add).then_inc(gn_dev, 1)
                until(dve, gn_dev, upto(2, i, 1 if g else 2))
                nc.vector.scalar_tensor_tensor(dev2[:, c], dev[:, c], dev[:, c], mv[:, g, 1:2], ALU.mult,
                                               ALU.add).then_inc(gn_stat, 1)

            def tap(i, n):
                t, part = divmod(n, 4)
                ty, tx = divmod(t, TAPS)
                r0 = part * (SIDE // 4)
                if n == 0:
                    until(dve, xp_ready, upto(1, i, 1))
                until(dve, tapped, upto(36, i, n - 3))
                a = ACC[:, r0:r0 + SIDE // 4, :]
                nc.vector.scalar_tensor_tensor(a, XP[:, r0 + ty:r0 + ty + SIDE // 4, tx:tx + SIDE], sg[:, t:t + 1], a,
                                               ALU.mult, ALU.add).then_inc(tapped, 1)

            add_at = {min(LAST[c] + LAG + 1, SLOTS - 1): c for c in range(3)}

            def body(i, s1, s2, cv):
                plan = [(at, soft, (i, what, h, n), soft_step, s2 if h else s1) for at, what, h, n in SOFT]
                plan += [(4 + k // 2, channel_stats, (i, 1, k), gn_chunk, cv) for k in range(7)]
                plan += [(8, channel_means, (i, 1), gn_stat, cv), (10, group_dev, (i, 1), gn_stat, cv)]
                plan += [(14 + k // 4, channel_stats, (i, 0, k), gn_chunk, s1) for k in range(7)]
                plan += [(16, channel_means, (i, 0), gn_stat, s1), (18, group_dev, (i, 0), gn_stat, s1)]
                plan += [(at, tap, (i, n), tapped, cv) for n, at in enumerate(TAP_SLOTS)]
                for g in range(BODY):
                    h, s = divmod(g, SLOTS)
                    if g == 8 and cv:
                        until(dve, gn_chunk, upto(14, i, 7))
                    if g == 16 and s1:
                        until(dve, gn_chunk, upto(14, i, 14))
                    if s2:
                        product(i, g)
                    elif s == 0 and s1:
                        skip(dve, prod_ready, SLOTS)
                        skip(dve, y_added, 4)
                    if s2 and s in add_at:
                        add_class(i, h, add_at[s])
                    if s == 2 and (s2 if h else cv):
                        add_class(i if h else i - 1, 1 - h, 3)
                    for at, do, what, sm, on in plan:
                        if at == g:
                            if on:
                                do(*what)
                            else:
                                if do is group_dev:
                                    skip(dve, gn_dev)
                                skip(dve, sm)

            steps(dve, body)

        @block.tensor
        def _(pe):
            pe.wait_ge(weights_in, 16 * N_W)
            pe.wait_ge(weights_up, 2)
            pe.wait_ge(pads_zero, N_PADS)

            def fill_use(i, n, kind, which, k):
                bank = side[n % 2]
                until(pe, side_read, upto(N_USES, i, n - 1))
                if kind == V:
                    h = which
                    r0, r1 = V_CUTS[h][k], V_CUTS[h][k + 1]
                    if k == 0:
                        until(pe, xn_ready, upto(2, i, 0) if h else upto(2, i, 1))
                    last = nc.tensor.matmul(bank[0:CH, 0:(r1 - r0) * SIDE], wv[:, :], XN[:, r0:r1, :],
                                            start=True, stop=True)
                elif kind == LOG:
                    h = which
                    if k == 0:
                        until(pe, pool_step, upto(4, i, 2 * h + 2))
                    last = nc.tensor.matmul(bank[0:QN, 0:ROWS[h] * WIN], wa[:, k, :, :],
                                            pooled[:, 0:ROWS[h], :], start=True, stop=True)
                elif kind == IN:
                    if k == 0:
                        until(pe, x_in, 16 * (i + 2))
                    for t in range(4):
                        last = nc.tensor.transpose(bank[0:CH, t * TP:(t + 1) * TP], tok_in[:, 4 * k + t, :], idn[:, :])
                elif kind == OUT:
                    if k == 0:
                        until(pe, tapped, upto(36, i, 36))
                    for t in range(4):
                        last = nc.tensor.transpose(bank[0:TP, t * CH:(t + 1) * CH], ACCt[:, 4 * k + t, :],
                                                   idn[0:CH, 0:CH])
                else:
                    g = which - 1
                    until(pe, gn_stat, upto(4, i, (0 if g else 2) + (1 if kind == GA else 2)))
                    src = mv[:, g, 0:1] if kind == GA else dev2[:, g:g + 1]
                    last = nc.tensor.matmul(bank[0:CH, 0:1], grp[:, :], src, start=True, stop=True)
                last.then_inc(side_full, 1)

            def broadcast(i, g):
                h, s = divmod(g, SLOTS)
                if s == 0:
                    until(pe, stacked[h], RESTACK * (i + 1))
                until(pe, prod_ready, upto(BODY, i, g - 1))
                for a in range(2):
                    _, _, _, who = TERMS[2 * s + a]
                    for n, ((si, qi, ki), (sj, qj, kj), which) in enumerate(who):
                        last = nc.tensor.matmul(
                            bc[g % 2][0:CH, a, 0:UNIT], sel[:, which, :],
                            stack[h][:, qi, ki * TAPS + kj, si:si + HALF, sj:sj + WIN],
                            start=(n == 0), stop=(n == len(who) - 1))
                last.then_inc(bcast_full, 1)

            def add_up(i, g):
                h, s = divmod(g, SLOTS)
                if s in PRE:
                    until(pe, pre_added, upto(2 * len(PRE), i, pre_no(g)))
                else:
                    until(pe, prod_ready, upto(BODY, i, g + 1))
                for a in range(1 if s in PRE else 2):
                    t = 2 * s + a
                    c = TERMS[t][0]
                    first = t == 0 or TERMS[t - 1][0] != c
                    if first:
                        until(pe, y_added, upto(8, i, 4 * h + c - 1))
                    last = nc.tensor.matmul(acc[c % 2][0:CH, 0:UNIT], wo[:, :], prod[:, g % PRODUCTS, a, :],
                                            start=first, stop=s == LAST[c] and (s in PRE or t == 2 * s + 1 or TERMS[t + 1][0] != c))
                last.then_inc(summed, 1)

            def body(i, s1, s2, cv):
                for g in range(BODY):
                    h, s = divmod(g, SLOTS)
                    if s2:
                        broadcast(i, g)
                        if g >= LAG:
                            add_up(i, g - LAG)
                    elif s1 and s == 0:
                        skip(pe, bcast_full, SLOTS)
                        skip(pe, summed, SLOTS)
                    if g < LAG and cv:
                        add_up(i - 1, BODY + g - LAG)
                    for n, (at, kind, which, k) in enumerate(USES):
                        if at == g:
                            if use_on(kind, which, s1, s2, cv):
                                fill_use(i, n, kind, which, k)
                            else:
                                skip(pe, side_full)

            steps(pe, body)


_INS = ["x", "L0_conv_W_v", "L0_conv_W_a", "L0_conv_b_a", "L0_conv_W_o", "L0_conv_b_o", "L1_conv_w"]


def kernel(**inputs):
    import numpy as np
    from concourse import bacc
    from concourse.bass_utils import run_bass_kernel_spmd

    ident = np.eye(TP, dtype=np.float32)
    chan = np.arange(CH)
    group = np.where(chan[:, None] // GROUP == chan[None, :] // GROUP, np.float32(-1.0 / GROUP), np.float32(0.0))
    row = np.arange(STACKED)
    shifted = row >= PARTS * PN
    head = row % HEADS == chan[:, None] // DIM
    column = np.where(shifted, TAPS, row // HEADS % TAPS)
    fed = [column == q for q in range(TAPS)] + [(column == TAPS - 1) | shifted]
    select = np.ascontiguousarray((np.stack(fed)[:, None, :] & head[None]).transpose(2, 0, 1)) * np.float32(1 / PART_UP)

    nc = bacc.Bacc("TRN2", target_bir_lowering=False, num_devices=1)
    arrays, args = {}, []
    for name in _INS:
        arrays["in_" + name] = np.ascontiguousarray(inputs[name])
    arrays["in_L1_conv_w"] = np.ascontiguousarray(np.asarray(inputs["L1_conv_w"]).reshape(KK, CH).T)
    arrays["ident"], arrays["group"], arrays["select"] = ident, group, select
    for name, a in arrays.items():
        args.append(nc.dram_tensor(name, a.shape, mybir.dt.from_np(a.dtype), kind="ExternalInput").ap())
    args.append(nc.dram_tensor("out", (BATCH, SIDE, SIDE, CH), mybir.dt.float32, kind="ExternalOutput").ap())
    build_program(nc, *args)
    r = run_bass_kernel_spmd(nc, [arrays], core_ids=[0])
    return r.results[0]["out"]
```

```python
import concourse.bass as bass
from concourse import mybir
from contextlib import ExitStack

BATCH, SIDE, CH = 32, 56, 96
HEADS, DIM, TAPS = 12, 8, 3
GROUP = 3
WIN = SIDE // 2
GRID = WIN + 1
PIX = SIDE * SIDE
PAD_P = SIDE + 2
PAD_V = SIDE + 3
TP, TT = 112, PIX // 112
HALF = WIN // 2
UNIT = HALF * WIN
ROWS = (HALF + 1, HALF)
PIX0 = (0, SIDE // 2 - 1)
PIXN = (SIDE // 2 + 2, SIDE // 2 + 1)
V_ROWS = 2 * (HALF - 1) + 5
KK = TAPS * TAPS
QN = KK * HEADS
PN = TAPS * HEADS
SCALE = float(DIM) ** -0.5

AXIS = {
    0: [(0, [(0, 1, 0)]), (1, [(0, 1, 1)]), (2, [(0, 1, 2)])],
    1: [(0, [(0, 2, 0)]), (1, [(0, 2, 1)]), (2, [(0, 2, 2), (1, 0, 0)]), (3, [(1, 0, 1)]), (4, [(1, 0, 2)])],
}
CLASSES = [(1, 1), (1, 0), (0, 1), (0, 0)]
TERMS = [(c, rv, cv, [(r, cols[0], TAPS if len(cols) == 2 else cols[0][1]) for r in rows])
         for c, (pr, pc) in enumerate(CLASSES) for rv, rows in AXIS[pr] for cv, cols in AXIS[pc]]
SLOTS = len(TERMS) // 2
LAST = [max(n for n, t in enumerate(TERMS) if t[0] == c) // 2 for c in range(4)]
BODY = 2 * SLOTS
LAG = 3
PRODUCTS = 4
V_CUTS = ((0, 8, 16, 23, 30), (0, 8, 15, 22, 29))

PARTS = 2
STACKED = PARTS * (TAPS + 1) * HEADS
SELS = TAPS + 1
PART_UP = 4096.0
V, LOG, IN, OUT, GA, GB = "values", "logits", "in", "out", "mean", "variance"
MAX, SUM, INV = "maximum", "sum", "inverse"
SUB, MUL, LOW = "less the maximum", "times the inverse", "second part"
EXP, UP, HIGH = "exponential", "scaled up", "first part"
AT = {
    "not pre": (0, 3, 8, 9, 10, 14, 15, 16, 22, 28, 33, 39, 46, 51, 54),
    V: ((27, 30, 33, 33), (62, 63, 65, 67)),
    LOG: ((19, 19, 21, 21, 21, 22, 22, 23, 23), (39, 39, 42, 43, 48, 48, 48, 51, 53)),
    IN: (5, 7, 7, 8, 9, 10, 10),
    OUT: (55, 56, 56, 57, 59, 59, 60),
    GA: (13, 5),
    GB: (17, 10),
    "gn scale": (15, 9),
    "squares": (13, 7),
    "pooled": (9, 34),
    "pool normed": (17, 37),
    MAX: ((24, 24, 27, 27), (56, 57, 57, 58)),
    SUB: ((26, 27, 28, 29, 30, 30, 32, 33, 34), (58, 59, 59, 62, 64, 64, 64, 65, 66)),
    EXP: ((33, 36, 37), (64, 65, 67)),
    SUM: ((36, 37, 38, 39), (70, 71, 73, 73)),
    INV: ((41, 43), (74, 75)),
    UP: ((42,), (76,)),
    MUL: ((44, 44, 45, 46, 47, 47, 48, 48, 49), (75, 76, 77, 78, 78, 79, 82, 83, 84)),
    HIGH: ((47, 48, 49), (81, 83, 86)),
    LOW: ((48, 49, 51, 51, 52, 52, 53, 54, 54), (81, 81, 84, 84, 85, 87, 88, 88, 88)),
    "normed": (18, 33),
    "start x1": 4,
    "start acc": 1,
    "rimmed": 10,
    "centred": (12, 14, 15),
    "taps": (14, 17, 18, 18, 19, 20, 20, 21, 25, 29, 30, 31, 32, 34, 35, 45, 48, 48, 48, 50, 50, 52, 53, 53),
}
PRE = [g for g in range(BODY)
       if TERMS[2 * (g % SLOTS)][0] == TERMS[2 * (g % SLOTS) + 1][0] and g not in AT["not pre"]]
CUTS = (0, 19, 38, SIDE)
TAP_N = 3 * (KK - 1)
assert len(AT["taps"]) == TAP_N


def pieces(*kinds):
    return sorted([(at % BODY, at // BODY, kind, h, n) for kind in kinds for h in range(2)
                   for n, at in enumerate(AT[kind][h])], key=lambda p: p[0])


USES = sorted(pieces(V, LOG) + [(at, 0, kind, g, 0) for kind in (GA, GB) for g, at in enumerate(AT[kind])]
              + [(at, 0, kind, 0, n) for kind in (IN, OUT) for n, at in enumerate(AT[kind])], key=lambda p: p[0])
assert len(USES) % 2 == 0
SOFT = pieces(MAX, SUM, INV)
FINE = pieces(SUB, MUL, LOW)
SMOOTH = pieces(EXP, UP, HIGH)


def done(listed, home, *what):
    n = next(n for n, p in enumerate(listed) if p[2:] == what)
    return upto(len(listed), home + listed[n][1], n + 1)


def upto(per_body, i, n):
    return (i + 1) * per_body + n


def build_program(nc, x, W_v, W_a, b_a, W_o, b_o, w_conv, ident, group, select, out):
    F32, F16 = mybir.dt.float32, mybir.dt.float16
    ALU, ACT, AX = mybir.AluOpType, mybir.ActivationFunctionType, mybir.AxisListType
    ctx = ExitStack()
    with ctx:
        def sb(name, shape, dt=F32):
            return ctx.enter_context(nc.sbuf_tensor(name, shape, dt))

        def sem(name):
            return ctx.enter_context(nc.semaphore(name))

        idn = sb("idn", [TP, TP])
        grp = sb("grp", [CH, CH])
        sel = sb("sel", [STACKED, SELS, CH], F16)
        wv = sb("wv", [CH, CH])
        wo = sb("wo", [CH, CH])
        wa = sb("wa", [CH, KK, KK, HEADS])
        ba = sb("ba", [QN, KK])
        bo = sb("bo", [CH, 1])
        wc = sb("wc", [CH, KK])
        sg = sb("sg", [CH, KK])
        sg2 = sb("sg2", [CH, KK])
        half_neg = sb("half_neg", [CH, 1])
        eps = sb("eps", [CH, 1])
        quarter = sb("quarter", [CH, 1])
        one = sb("one", [CH, 1])
        centre = sb("centre", [CH, 3])
        tok_in = sb("tok_in", [TP, TT, CH])
        tok_out = sb("tok_out", [TP, 2, 4, CH])
        X0 = sb("X0", [CH, PIX])
        XN = sb("XN", [CH, PIXN[0], SIDE])
        X1 = sb("X1", [CH, SIDE, SIDE])
        ACC = sb("ACC", [CH, SIDE, SIDE])
        XP = sb("XP", [CH, PAD_P, PAD_P])
        VAL = [sb(f"VAL{h}", [CH, V_ROWS, PAD_V]) for h in range(2)]
        pc = sb("pc", [CH, PIXN[0], WIN])
        pooled = sb("pooled", [CH, ROWS[0], WIN])
        att = [sb(f"att{h}", [QN, KK, ROWS[h] * WIN]) for h in range(2)]
        top = [sb(f"top{h}", [QN, ROWS[h] * WIN]) for h in range(2)]
        parts = [sb(f"part{p}", [QN, KK, ROWS[0], GRID], F16) for p in range(PARTS)]
        stack = [sb(f"stack{h}", [STACKED, TAPS, KK, HALF + 1, GRID], F16) for h in range(2)]
        prod = sb("prod", [CH, PRODUCTS, 2, UNIT])
        sums = sb("sums", [CH, 2, 7])
        squares = sb("squares", [CH, 2, 2])
        spill = sb("spill", [CH, 7])
        nmean = sb("nmean", [CH, 2])
        gvar = sb("gvar", [CH, 2])
        gve = sb("gve", [CH, 2])
        rstd = sb("rstd", [CH, 2])
        rstd_4 = sb("rstd_4", [CH, 1])
        shift = sb("shift", [CH, 2])

        bc = [ctx.enter_context(nc.psum_tensor(f"bc{b}", [128, 2, 512], F32)) for b in range(2)]
        acc = [ctx.enter_context(nc.psum_tensor(f"acc{b}", [128, 512], F32)) for b in range(2)]
        side = [ctx.enter_context(nc.psum_tensor(f"side{b}", [128, 512], F32)) for b in range(2)]

        weights_in = sem("weights_in")
        weights_up = sem("weights_up")
        pads_zero = sem("pads_zero")
        rims_zero = sem("rims_zero")
        bcast_full = sem("bcast_full")
        prod_ready = sem("prod_ready")
        summed = sem("summed")
        y_added = sem("y_added")
        side_full = sem("side_full")
        side_read = sem("side_read")
        xn_ready = sem("xn_ready")
        pool_step = sem("pool_step")
        pool_normed = sem("pool_normed")
        soft_step = sem("soft_step")
        fine_step = sem("fine_step")
        smooth_step = sem("smooth_step")
        pre_added = sem("pre_added")
        stacked = [sem(f"stacked{h}") for h in range(2)]
        gn_square = sem("gn_square")
        gn_scale = sem("gn_scale")
        acc_init = sem("acc_init")
        x1_init = sem("x1_init")
        xp_ready = sem("xp_ready")
        centred = sem("centred")
        tapped = sem("tapped")
        x_in = sem("x_in")
        y_out = [sem(f"y_out{b}") for b in range(2)]

        N_W = 8 + KK
        N_PADS = 4 + 2 + PARTS
        RESTACK = 16 * 4 * PARTS * TAPS // 2
        x_v = x.rearrange("b h w c -> b (h w) c").rearrange("b (p t) c -> b p t c", t=TT)
        out_v = out.rearrange("b h w c -> b (h w) c").rearrange("b (p t) c -> b p t c", t=TT)
        X0t = X0[:, :].rearrange("c (p t) -> c t p", t=TT)
        ACCf = ACC[:, :, :].rearrange("c h w -> c (h w)")
        ACCt = ACCf.rearrange("c (p t) -> c t p", t=TT)
        X0i = X0[:, :].rearrange("c (h w) -> c h w", w=SIDE)

        wa_in = X1[:, :, :].rearrange("c h w -> c (h w)")[:, 0:KK * QN]
        sel_in = ACCf[0:STACKED, 0:SELS * CH].rearrange("r (s c) -> r s c", c=CH)

        def a4(h):
            return att[h][:, :, :].rearrange("r k (i j) -> r k i j", j=WIN)

        def use_on(use, s1, s2, cv):
            _, late, kind, which, _ = use
            if kind == OUT or (kind in (GA, GB) and which == 1):
                return cv
            return s2 if late else s1

        def chunks(kind, g):
            return 1 if g else (7 if kind == GA else 2)

        def store_no(i, k):
            return 16 * ((4 - k % 2) * (i - 1) + k // 2 + 1)

        def until(eng, sm, value):
            if not isinstance(value, int) or value > 0:
                eng.wait_ge(sm, value)

        def skip(eng, sm, n=1):
            eng.drain().then_inc(sm, n)

        def steps(eng, body):
            body(-1, True, False, False)
            body(0, True, True, False)
            with eng.Fori(1, BATCH - 1) as i:
                body(i, True, True, True)
            body(BATCH - 1, False, True, True)
            body(BATCH, False, False, True)

        block = ctx.enter_context(nc.Block())

        @block.sync
        def _(sp):
            for dst, src in ((idn[:, :], ident), (grp[:, :], group), (wv[:, :], W_v), (wo[:, :], W_o),
                             (bo[:, :], b_o.rearrange("(c o) -> c o", o=1)),
                             (wa_in, W_a)):
                sp.dma_start(dst, src).then_inc(weights_in, 16)
            sp.dma_start(sel_in, select).then_inc(weights_in, 16)
            ba_v = b_a.rearrange("(n q k) -> q n k", n=HEADS, q=KK)
            for q in range(KK):
                sp.dma_start(ba[q * HEADS:(q + 1) * HEADS, :], ba_v[q]).then_inc(weights_in, 16)
            sp.dma_start(wc[:, :], w_conv).then_inc(weights_in, 16)
            for b in range(2):
                sp.sem_inc(y_out[b], 16)

            def restack(home, h):
                for p, (sm, listed, last) in enumerate(((smooth_step, SMOOTH, (HIGH, h, 2)),
                                                        (fine_step, FINE, (LOW, h, KK - 1)))):
                    until(sp, sm, done(listed, home, *last))
                    for q in range(TAPS):
                        sp.dma_start(stack[h][p * PN:(p + 1) * PN, q, :, 0:ROWS[h], :],
                                     parts[p][q * PN:(q + 1) * PN, :, 0:ROWS[h], :]).then_inc(stacked[h], 16)
                        row = PARTS * PN + p * HEADS
                        n = ROWS[h] * GRID - 1
                        sp.dma_start(
                            stack[h][row:row + HEADS, q].rearrange("r (a b) i j -> r a b (i j)", b=TAPS)[:, :, 2, 0:n],
                            parts[p][q * PN:q * PN + HEADS].rearrange("r (a b) i j -> r a b (i j)", b=TAPS)[:, :, 0, 1:n + 1],
                        ).then_inc(stacked[h], 16)

            def body(i, s1, s2, cv):
                if s1:
                    until(sp, side_full, done(USES, i - 1, IN, 0, 6))
                    sp.dma_start(tok_in[:, :, :], x_v[i + 1]).then_inc(x_in, 16)
                if not s2 and not cv:
                    sp.wait_ge(rims_zero, 2)
                if s2:
                    restack(i - 1, 1)
                if s1:
                    restack(i, 0)

            steps(sp, body)
            for b in range(2):
                sp.wait_ge(y_out[b], store_no(BATCH + 1, b))

        @block.gpsimd
        def _(pool):
            nc.gpsimd.memset(half_neg[:, :], -0.5).then_inc(pads_zero, 1)
            nc.gpsimd.memset(quarter[:, :], 0.25).then_inc(pads_zero, 1)
            nc.gpsimd.memset(one[:, :], 1.0).then_inc(pads_zero, 1)
            nc.gpsimd.memset(eps[:, :], 1e-5).then_inc(pads_zero, 1)
            for h in range(2):
                nc.gpsimd.memset(VAL[h][:, :, :], 0.0).then_inc(pads_zero, 1)
            for p in range(PARTS):
                nc.gpsimd.memset(parts[p][:, :, :, :], 0.0).then_inc(pads_zero, 1)
            pool.wait_ge(pads_zero, N_PADS)
            pool.wait_ge(weights_up, 8)

            def pooling(i, h):
                n = 0 if h == 0 else 2
                until(pool, side_read, done(USES, i, IN, 0, 6))
                until(pool, pool_step, upto(4, i, n))
                r0 = 2 * (HALF if h else 0)
                nr = 2 * min(ROWS[h], WIN)
                xv = X0i[:, r0:r0 + nr, :].rearrange("c r (w two) -> c r w two", two=2)
                nc.gpsimd.tensor_tensor(pc[:, 0:nr, :], xv[:, :, :, 0], xv[:, :, :, 1],
                                        ALU.add).then_inc(pool_step, 1)
                until(pool, pool_step, upto(4, i, n + 1))
                until(pool, side_full, done(USES, i if h else i - 1, LOG, 1 - h, KK - 1))
                pv = pc[:, 0:nr, :].rearrange("c (r two) w -> c r two w", two=2)
                nc.gpsimd.tensor_tensor(pooled[:, 0:ROWS[h], :], pv[:, :, 0, :], pv[:, :, 1, :],
                                        ALU.add).then_inc(pool_step, 1)

            def fine(home, what, h, k):
                if what == SUB:
                    if k == 0:
                        until(pool, soft_step, done(SOFT, home, MAX, h, 3))
                    nc.gpsimd.tensor_tensor(att[h][:, k, :], att[h][:, k, :], top[h][:, :],
                                            ALU.subtract).then_inc(fine_step, 1)
                elif what == MUL:
                    if k == 0:
                        until(pool, smooth_step, done(SMOOTH, home, UP, h, 0))
                    nc.gpsimd.tensor_tensor(att[h][:, k, :], att[h][:, k, :], top[h][:, :],
                                            ALU.mult).then_inc(fine_step, 1)
                else:
                    until(pool, smooth_step, done(SMOOTH, home, HIGH, h, k // 3))
                    low, high = (parts[p][:, k, 0:ROWS[h], 0:WIN] for p in (1, 0))
                    nc.gpsimd.tensor_tensor(low, a4(h)[:, k], high,
                                            ALU.subtract).then_inc(fine_step, 1)

            def pre_add(i, g):
                until(pool, prod_ready, upto(BODY, i, g + 1))
                p = prod[:, g % PRODUCTS, :, :]
                nc.gpsimd.tensor_tensor(p[:, 0, :], p[:, 0, :], p[:, 1, :], ALU.add).then_inc(pre_added, 1)

            def norm_scale(i, g):
                n = 0 if g else 6
                c = slice(g, g + 1)
                until(pool, side_read, done(USES, i, GB, g, 0))
                nc.gpsimd.tensor_tensor(gve[:, c], eps[:, :], gvar[:, c], ALU.subtract).then_inc(gn_scale, 1)
                until(pool, gn_scale, upto(10, i, n + 1))
                nc.gpsimd.tensor_tensor(rstd[:, c], gve[:, c], half_neg[:, :], ALU.pow).then_inc(gn_scale, 1)
                until(pool, gn_scale, upto(10, i, n + 2))
                nc.gpsimd.tensor_tensor(shift[:, c], nmean[:, c], rstd[:, c], ALU.mult).then_inc(gn_scale, 1)
                if g:
                    s = sg[:, KK // 2:KK // 2 + 1]
                    nc.gpsimd.tensor_tensor(centre[:, 0:1], s, rstd[:, c], ALU.mult).then_inc(gn_scale, 1)
                    until(pool, gn_scale, upto(10, i, n + 4))
                    nc.gpsimd.tensor_tensor(centre[:, 1:2], centre[:, 0:1], one[:, :], ALU.add).then_inc(gn_scale, 1)
                    nc.gpsimd.tensor_tensor(centre[:, 2:3], s, shift[:, c], ALU.mult).then_inc(gn_scale, 1)
                else:
                    nc.gpsimd.tensor_tensor(rstd_4[:, :], rstd[:, c], quarter[:, :], ALU.mult).then_inc(gn_scale, 1)

            def body(i, s1, s2, cv):
                for g in range(BODY):
                    h, s = divmod(g, SLOTS)
                    if g in PRE:
                        if s2:
                            pre_add(i, g)
                        elif g == PRE[0]:
                            skip(pool, pre_added, len(PRE))
                    for at, late, *what in FINE:
                        if at == g:
                            if s2 if late else s1:
                                fine(i - late, *what)
                            else:
                                skip(pool, fine_step)
                    for at, do, sm, n, which in ((AT["gn scale"][1], lambda: norm_scale(i, 1), gn_scale, 6, cv),
                                                 (AT["gn scale"][0], lambda: norm_scale(i, 0), gn_scale, 4, s1),
                                                 (AT["pooled"][0], lambda: pooling(i, 0), pool_step, 2, s1),
                                                 (AT["pooled"][1], lambda: pooling(i, 1), pool_step, 2, s1)):
                        if at == g:
                            if which:
                                do()
                            else:
                                skip(pool, sm, n)

            steps(pool, body)

        @block.scalar
        def _(act):
            act.wait_ge(weights_in, 16 * N_W)

            def read_use(i, n, late, kind, which, k):
                bank = side[n % 2]
                until(act, side_full, upto(len(USES), i, n + 1))
                if kind == V:
                    h = which
                    r0, r1 = V_CUTS[h][k], V_CUTS[h][k + 1]
                    if k == 0:
                        until(act, prod_ready, upto(BODY, i - late, BODY if h else SLOTS))
                    top_row = 1 - h
                    ins = nc.scalar.activation(
                        VAL[h][:, top_row + r0:top_row + r1, 1:1 + SIDE],
                        bank[0:CH, 0:(r1 - r0) * SIDE].rearrange("c (r w) -> c r w", w=SIDE), ACT.Identity)
                elif kind == LOG:
                    h, cols = which, ROWS[which] * WIN
                    until(act, fine_step, done(FINE, i - 1, LOW, h, k))
                    ins = nc.scalar.activation(att[h][:, k, :], bank[0:QN, 0:cols],
                                               ACT.Identity, bias=ba[:, k:k + 1])
                elif kind == IN:
                    if k == 0:
                        until(act, x1_init, upto(1, i, 1))
                        until(act, pool_step, upto(4, i, 0))
                    ins = nc.scalar.activation(X0t[:, 4 * k:4 * k + 4, :],
                                               bank[0:CH, 0:4 * TP].rearrange("c (t p) -> c t p", t=4), ACT.Identity,
                                               accum_out=sums[:, 0, k:k + 1])
                elif kind == OUT:
                    act.wait_ge(y_out[k % 2], store_no(i, k))
                    ins = nc.scalar.activation(tok_out[:, k % 2, :, :],
                                               bank[0:TP, 0:4 * CH].rearrange("p (t c) -> p t c", t=4), ACT.Identity)
                else:
                    g = which
                    n_in = chunks(kind, g)
                    ins = nc.scalar.activation(spill[:, 0:n_in], bank[0:CH, 0:n_in], ACT.Identity,
                                               accum_out=(nmean if kind == GA else gvar)[:, g:g + 1])
                ins.then_inc(side_read, 1)

            def store(i, k):
                until(act, side_read, done(USES, i, OUT, 0, k))
                act.dma_start(out_v[i - 1, :, 4 * k:4 * k + 4, :], tok_out[:, k % 2, :, :]).then_inc(y_out[k % 2], 16)

            def smooth(home, what, h, n):
                if what == EXP:
                    a = att[h][:, 3 * n:3 * n + 3, :]
                    until(act, fine_step, done(FINE, home, SUB, h, 3 * n + 2))
                    ins = nc.scalar.activation(a, a, ACT.Exp, scale=SCALE)
                elif what == UP:
                    until(act, soft_step, done(SOFT, home, INV, h, 1))
                    ins = nc.scalar.activation(top[h][:, :], top[h][:, :], ACT.Identity, scale=PART_UP)
                else:
                    until(act, fine_step, done(FINE, home, MUL, h, 3 * n + 2))
                    if n == 0:
                        until(act, stacked[1 - h], RESTACK * (home + 1 + h))
                        until(act, bcast_full, upto(BODY, home, BODY if h else SLOTS))
                    ins = nc.scalar.activation(parts[0][:, 3 * n:3 * n + 3, 0:ROWS[h], 0:WIN], a4(h)[:, 3 * n:3 * n + 3],
                                               ACT.Identity)
                ins.then_inc(smooth_step, 1)

            def normed(i, h):
                if h == 0:
                    until(act, gn_scale, upto(10, i, 10))
                until(act, side_read, done(USES, i if h else i - 1, V, 1 - h, 3))
                rows = slice(PIX0[h], PIX0[h] + PIXN[h])
                nc.scalar.activation(XN[:, 0:PIXN[h], :], X0i[:, rows, :], ACT.Identity,
                                     bias=shift[:, 0:1], scale=rstd[:, 0:1]).then_inc(xn_ready, 1)

            def pool_norm(i, h):
                until(act, gn_scale, upto(10, i, 10))
                until(act, pool_step, upto(4, i, 2 * h + 2))
                p = pooled[:, 0:ROWS[h], :]
                nc.scalar.activation(p, p, ACT.Identity, bias=shift[:, 0:1],
                                     scale=rstd_4[:, :]).then_inc(pool_normed, 1)

            def start_acc(i):
                until(act, y_added, upto(8, i, 0))
                nc.scalar.activation(ACC[:, :, :], X1[:, :, :], ACT.Identity,
                                     accum_out=sums[:, 1, 0:1]).then_inc(acc_init, 1)

            def square_1(i):
                until(act, side_read, done(USES, i, GA, 1, 0))
                until(act, tapped, upto(TAP_N, i, 0))
                nc.scalar.activation(XP[:, 1:1 + SIDE, 1:1 + SIDE], ACC[:, :, :], ACT.Square, bias=nmean[:, 1:2],
                                     accum_out=squares[:, 1, 0:1]).then_inc(gn_square, 1)

            def square_0(i, n):
                if n == 0:
                    until(act, side_read, done(USES, i, GA, 0, 0))
                    until(act, side_read, done(USES, i - 1, V, 1, 3))
                else:
                    until(act, gn_square, upto(3, i, 2))
                rows = slice(n * WIN, (n + 1) * WIN)
                nc.scalar.activation(XN[:, 0:WIN, :], X0i[:, rows, :], ACT.Square, bias=nmean[:, 0:1],
                                     accum_out=squares[:, 0, n:n + 1]).then_inc(gn_square, 1)

            def start_x1(i):
                until(act, acc_init, upto(1, i, 1))
                until(act, side_read, done(USES, i - 1, IN, 0, 6))
                nc.scalar.activation(X1[:, :, :], X0i, ACT.Identity, bias=bo[:, 0:1]).then_inc(x1_init, 1)

            def rimmed(i):
                until(act, gn_scale, upto(10, i, 3))
                nc.scalar.activation(XP[:, 1:1 + SIDE, 1:1 + SIDE], ACC[:, :, :], ACT.Identity,
                                     bias=shift[:, 1:2], scale=rstd[:, 1:2]).then_inc(xp_ready, 1)

            def centre_tap(i, part):
                until(act, gn_scale, upto(10, i, 6))
                until(act, xp_ready, upto(1, i, 1))
                a = ACC[:, CUTS[part]:CUTS[part + 1], :]
                nc.scalar.activation(a, a, ACT.Identity, bias=centre[:, 2:3], scale=centre[:, 1:2]).then_inc(centred, 1)

            def body(i, s1, s2, cv):
                more = [(at, smooth, (i - late, *what), smooth_step, s2 if late else s1) for at, late, *what in SMOOTH]
                more += [(AT["squares"][0], square_0, (i, n), gn_square, s1) for n in range(2)]
                more += [(AT["start acc"], start_acc, (i,), acc_init, cv),
                         (AT["start x1"], start_x1, (i,), x1_init, s2),
                         (AT["squares"][1], square_1, (i,), gn_square, cv),
                         *((at, centre_tap, (i, n), centred, cv) for n, at in enumerate(AT["centred"])),
                         (AT["rimmed"], rimmed, (i,), xp_ready, cv),
                         *((AT["pool normed"][h], pool_norm, (i, h), pool_normed, s1) for h in range(2))]
                more += [(AT["normed"][h], normed, (i, h), xn_ready, s1) for h in range(2)]
                for g in range(BODY):
                    if g == AT[V][0][0] and not s2 and not cv:
                        act.wait_ge(pads_zero, N_PADS)
                    for n, use in enumerate(USES):
                        if use[0] == g:
                            if use_on(use, s1, s2, cv):
                                read_use(i, n, *use[1:])
                            else:
                                skip(act, side_read)
                            if use[2] == OUT and cv:
                                store(i, use[4])
                    for at, do, what, sm, on in more:
                        if at == g:
                            if on:
                                do(*what)
                            else:
                                skip(act, sm)

            steps(act, body)

        @block.vector
        def _(dve):
            dve.wait_ge(weights_in, 16 * N_W)
            nc.vector.tensor_copy(wa[:, :, :, :], wa_in.rearrange("c (n q k) -> c k q n", n=HEADS, q=KK)).then_inc(
                weights_up, 1)
            nc.vector.tensor_copy(sel[:, :, :], sel_in).then_inc(weights_up, 1)
            nc.vector.tensor_scalar(wc[:, :], wc[:, :], -1.0, 1.0, ALU.max, ALU.min).then_inc(weights_up, 1)
            dve.wait_ge(weights_up, 3)
            nc.vector.tensor_scalar(sg[:, :], wc[:, :], 0.0, None, ALU.is_gt).then_inc(weights_up, 1)
            nc.vector.tensor_scalar(sg2[:, :], wc[:, :], 0.0, None, ALU.is_lt).then_inc(weights_up, 1)
            dve.wait_ge(weights_up, 5)
            nc.vector.tensor_tensor(sg[:, :], sg[:, :], sg2[:, :], ALU.subtract).then_inc(weights_up, 1)
            dve.wait_ge(weights_up, 6)
            nc.vector.tensor_tensor(sg[:, :], sg[:, :], wc[:, :], ALU.subtract).then_inc(weights_up, 1)
            dve.wait_ge(weights_up, 7)
            nc.vector.tensor_tensor(sg[:, :], sg[:, :], wc[:, :], ALU.add).then_inc(weights_up, 1)
            for h in range(2):
                nc.vector.memset(stack[h][:, :, :, :, :], 0.0).then_inc(rims_zero, 1)
            nc.vector.memset(XP[:, :, :], 0.0).then_inc(rims_zero, 1)
            dve.wait_ge(weights_up, 8)

            def product(i, g):
                h, s = divmod(g, SLOTS)
                if s == 0:
                    until(dve, side_read, done(USES, i - 1, V, h, 3))
                (_, r0, c0, _), (_, r1, c1, _) = TERMS[2 * s:2 * s + 2]
                v0 = VAL[h][:, r0:r0 + 2 * HALF - 1:2, c0:c0 + 2 * WIN - 1:2]
                v = bass.AP(v0.tensor, v0.offset, [v0.ap[0], [(r1 - r0) * PAD_V + c1 - c0, 2], *v0.ap[1:]])
                until(dve, bcast_full, upto(BODY, i, g + 1))
                until(dve, summed, upto(BODY, i, g + 1 - PRODUCTS))
                b = bc[g % 2][0:CH, :, 0:UNIT].rearrange("c a (i j) -> c a i j", j=WIN)
                nc.vector.tensor_tensor(prod[:, g % PRODUCTS, :, :].rearrange("c a (i j) -> c a i j", j=WIN),
                                        b, v, ALU.mult).then_inc(prod_ready, 1)

            def add_class(i, h, c):
                until(dve, summed, upto(BODY, i, h * SLOTS + LAST[c] + 1))
                if h == 0 and c == 0:
                    until(dve, x1_init, upto(1, i, 1))
                pr, pq = CLASSES[c]
                r0 = 2 * HALF * h + pr
                xv = X1[:, r0:r0 + 2 * HALF - 1:2, pq:pq + 2 * WIN - 1:2]
                nc.vector.tensor_tensor(xv, acc[c % 2][0:CH, 0:UNIT].rearrange("c (i j) -> c i j", j=WIN), xv,
                                        ALU.add).then_inc(y_added, 1)

            def soft(home, what, h, n):
                w = ROWS[h] * WIN
                c = slice(n * w // 4, (n + 1) * w // 4)
                by_window = att[h][:, :, :].rearrange("r k n -> r n k")
                if what == MAX:
                    if n == 0:
                        until(dve, side_read, done(USES, home, LOG, h, KK - 1))
                        until(dve, fine_step, done(FINE, home - 1, MUL, h, KK - 1))
                    ins = nc.vector.tensor_reduce(top[h][:, c], by_window[:, c, :], AX.X, ALU.max)
                elif what == SUM:
                    if n == 0:
                        until(dve, smooth_step, done(SMOOTH, home, EXP, h, 2))
                    ins = nc.vector.tensor_reduce(top[h][:, c], by_window[:, c, :], AX.X, ALU.add)
                else:
                    c = slice(n * w // 2, (n + 1) * w // 2)
                    until(dve, soft_step, done(SOFT, home, SUM, h, 2 * n + 1))
                    ins = nc.vector.reciprocal(top[h][:, c], top[h][:, c])
                ins.then_inc(soft_step, 1)

            def tap(i, n):
                t, part = divmod(n, 3)
                t += t >= KK // 2
                ty, tx = divmod(t, TAPS)
                r0, r1 = CUTS[part], CUTS[part + 1]
                if n == 0:
                    until(dve, xp_ready, upto(1, i, 1))
                if n < 3:
                    until(dve, centred, upto(3, i, n + 1))
                else:
                    until(dve, tapped, upto(TAP_N, i, n - 2))
                a = ACC[:, r0:r1, :]
                nc.vector.scalar_tensor_tensor(a, XP[:, r0 + ty:r1 + ty, tx:tx + SIDE], sg[:, t:t + 1], a,
                                               ALU.mult, ALU.add).then_inc(tapped, 1)

            add_at = {min(LAST[c] + LAG + 1, SLOTS - 1): c for c in range(3)}

            def body(i, s1, s2, cv):
                plan = [(at, soft, (i - late, *what), soft_step, s2 if late else s1) for at, late, *what in SOFT]
                plan += [(at, tap, (i, n), tapped, cv) for n, at in enumerate(AT["taps"])]
                for g in range(BODY):
                    h, s = divmod(g, SLOTS)
                    if s2:
                        product(i, g)
                    elif s == 0 and s1:
                        skip(dve, prod_ready, SLOTS)
                        skip(dve, y_added, 4)
                    if s2 and s in add_at:
                        add_class(i, h, add_at[s])
                    if s == LAG - 1 and (s2 if h else cv):
                        add_class(i if h else i - 1, 1 - h, 3)
                    for at, do, what, sm, on in plan:
                        if at == g:
                            if on:
                                do(*what)
                            else:
                                skip(dve, sm)

            steps(dve, body)

        @block.tensor
        def _(pe):
            pe.wait_ge(weights_in, 16 * N_W)
            pe.wait_ge(weights_up, 2)

            def fill_use(i, n, late, kind, which, k):
                bank = side[n % 2]
                until(pe, side_read, upto(len(USES), i, n - 1))
                if kind == V:
                    h = which
                    r0, r1 = V_CUTS[h][k], V_CUTS[h][k + 1]
                    if k == 0:
                        until(pe, xn_ready, upto(2, i - late, h + 1))
                    last = nc.tensor.matmul(bank[0:CH, 0:(r1 - r0) * SIDE], wv[:, :], XN[:, r0:r1, :],
                                            start=True, stop=True)
                elif kind == LOG:
                    h = which
                    if k == 0:
                        until(pe, pool_normed, upto(2, i, h + 1))
                    last = nc.tensor.matmul(bank[0:QN, 0:ROWS[h] * WIN], wa[:, k, :, :],
                                            pooled[:, 0:ROWS[h], :], start=True, stop=True)
                elif kind == IN:
                    if k == 0:
                        until(pe, x_in, 16 * (i + 2))
                    for t in range(4):
                        last = nc.tensor.transpose(bank[0:CH, t * TP:(t + 1) * TP], tok_in[:, 4 * k + t, :], idn[:, :])
                elif kind == OUT:
                    if k == 0:
                        until(pe, tapped, upto(TAP_N, i, TAP_N))
                    for t in range(4):
                        last = nc.tensor.transpose(bank[0:TP, t * CH:(t + 1) * CH], ACCt[:, 4 * k + t, :],
                                                   idn[0:CH, 0:CH])
                else:
                    g = which
                    if kind == GB:
                        until(pe, gn_square, upto(3, i, 1 if g else 3))
                    elif g:
                        until(pe, acc_init, upto(1, i, 1))
                    else:
                        until(pe, side_read, done(USES, i, IN, 0, 6))
                    src = (sums if kind == GA else squares)[:, g, 0:chunks(kind, g)]
                    last = nc.tensor.matmul(bank[0:CH, 0:chunks(kind, g)], grp[:, :], src, start=True, stop=True)
                last.then_inc(side_full, 1)

            def broadcast(i, g):
                h, s = divmod(g, SLOTS)
                if s == 0:
                    until(pe, stacked[h], RESTACK * (i + 1))
                until(pe, prod_ready, upto(BODY, i, g - 1))
                for a in range(2):
                    _, _, _, who = TERMS[2 * s + a]
                    for n, ((si, qi, ki), (sj, qj, kj), which) in enumerate(who):
                        last = nc.tensor.matmul(
                            bc[g % 2][0:CH, a, 0:UNIT], sel[:, which, :],
                            stack[h][:, qi, ki * TAPS + kj, si:si + HALF, sj:sj + WIN],
                            start=(n == 0), stop=(n == len(who) - 1))
                last.then_inc(bcast_full, 1)

            def add_up(i, g):
                h, s = divmod(g, SLOTS)
                if g in PRE:
                    until(pe, pre_added, upto(len(PRE), i, PRE.index(g) + 1))
                else:
                    until(pe, prod_ready, upto(BODY, i, g + 1))
                for a in range(1 if g in PRE else 2):
                    t = 2 * s + a
                    c = TERMS[t][0]
                    first = t == 0 or TERMS[t - 1][0] != c
                    if first:
                        until(pe, y_added, upto(8, i, 4 * h + c - 1))
                    last = nc.tensor.matmul(acc[c % 2][0:CH, 0:UNIT], wo[:, :], prod[:, g % PRODUCTS, a, :],
                                            start=first, stop=s == LAST[c] and (
                                                g in PRE or t == 2 * s + 1 or TERMS[t + 1][0] != c))
                last.then_inc(summed, 1)

            def body(i, s1, s2, cv):
                for g in range(BODY):
                    h, s = divmod(g, SLOTS)
                    if s2:
                        broadcast(i, g)
                        if g >= LAG:
                            add_up(i, g - LAG)
                    elif s1 and s == 0:
                        skip(pe, bcast_full, SLOTS)
                        skip(pe, summed, SLOTS)
                    if g < LAG and cv:
                        add_up(i - 1, BODY + g - LAG)
                    for n, use in enumerate(USES):
                        if use[0] == g:
                            if use_on(use, s1, s2, cv):
                                fill_use(i, n, *use[1:])
                            else:
                                skip(pe, side_full)

            steps(pe, body)


_INS = ["x", "L0_conv_W_v", "L0_conv_W_a", "L0_conv_b_a", "L0_conv_W_o", "L0_conv_b_o", "L1_conv_w"]


def kernel(**inputs):
    import numpy as np
    from concourse import bacc
    from concourse.bass_utils import run_bass_kernel_spmd

    ident = np.eye(TP, dtype=np.float32)
    chan = np.arange(CH)
    group = np.where(chan[:, None] // GROUP == chan[None, :] // GROUP,
                     np.float32(-1.0 / (GROUP * PIX)), np.float32(0.0))
    row = np.arange(STACKED)
    shifted = row >= PARTS * PN
    head = row % HEADS == chan[:, None] // DIM
    column = np.where(shifted, TAPS, row // HEADS % TAPS)
    fed = [column == q for q in range(TAPS)] + [(column == TAPS - 1) | shifted]
    select = np.ascontiguousarray((np.stack(fed)[:, None, :] & head[None]).transpose(2, 0, 1)) * np.float32(1 / PART_UP)

    nc = bacc.Bacc("TRN2", target_bir_lowering=False, num_devices=1)
    arrays, args = {}, []
    for name in _INS:
        arrays["in_" + name] = np.ascontiguousarray(inputs[name])
    arrays["in_L1_conv_w"] = np.ascontiguousarray(np.asarray(inputs["L1_conv_w"]).reshape(KK, CH).T)
    arrays["ident"], arrays["group"], arrays["select"] = ident, group, select
    for name, a in arrays.items():
        args.append(nc.dram_tensor(name, a.shape, mybir.dt.from_np(a.dtype), kind="ExternalInput").ap())
    args.append(nc.dram_tensor("out", (BATCH, SIDE, SIDE, CH), mybir.dt.float32, kind="ExternalOutput").ap())
    build_program(nc, *args)
    r = run_bass_kernel_spmd(nc, [arrays], core_ids=[0])
    return r.results[0]["out"]
```
